# Optimizing a Trainium2 kernel written in Bass

```python
import numpy as np
import jax
import jax.numpy as jnp

def _softmax(x, axis=-1):
    return jax.nn.softmax(x, axis=axis)

def _gelu(x):
    return jax.nn.gelu(x, approximate=True)

def _silu(x):
    return jax.nn.silu(x)

def _sigmoid(x):
    return jax.nn.sigmoid(x)

def _layernorm(x, axis=-1, eps=1e-05):
    m = jnp.mean(x, axis=axis, keepdims=True)
    v = jnp.var(x, axis=axis, keepdims=True)
    return (x - m) / jnp.sqrt(v + eps)

def _scatter_add(tgt, idx, src, axis=0):
    return tgt.at[idx].add(src)

def _segment_sum(src, seg, n):
    return jax.ops.segment_sum(src, seg, n)
kernel_name = 'mk_flamingo_gated_d4_seqx_r8_534941'

def setup_inputs(seed: int=0):
    np.random.seed(seed)
    _w = jnp.asarray

    def _rec_inputs():
        import jax
        import jax.numpy as jnp
        _rk = jax.random.key(seed)
        x = -0.0003929 + 0.9999 * jax.random.normal(jax.random.fold_in(_rk, 1), (8, 128, 512), jnp.float32)
        _lenS = 128 - jax.random.randint(jax.random.fold_in(_rk, 7), (8,), 0, max(1, 128 // 4) + 1, jnp.int32)
        _lenS2 = 128 - jax.random.randint(jax.random.fold_in(_rk, 8), (8,), 0, max(1, 128 // 4) + 1, jnp.int32)
        _ctx_4096P = jax.random.normal(jax.random.fold_in(_rk, 11), (8, 16, 512), jnp.float32)
        _ctx_4096c = jax.random.dirichlet(jax.random.fold_in(_rk, 511), 0.3 * jnp.ones((16,), jnp.float32), (8, 128))
        _ctx_4096t = jnp.einsum('bsk,bkd->bsd', _ctx_4096c, _ctx_4096P)
        _ctx_4096t = _ctx_4096t * jax.lax.rsqrt(jnp.mean(jnp.square(_ctx_4096t)) + 1e-12) * 0.953939
        ctx_4096 = 2.81802e-05 + 1.00001 * (_ctx_4096t + 0.3 * jax.random.normal(jax.random.fold_in(_rk, 611), (8, 128, 512), jnp.float32))
        pos_BxS2 = jnp.broadcast_to(jnp.arange(128, dtype=jnp.int32), (8, 128))
        _validS = jnp.arange(128)[None, :] < _lenS[:, None]
        _validS2 = jnp.arange(128)[None, :] < _lenS2[:, None]
        _causal = jnp.tril(jnp.ones((128, 128), dtype=bool))
        mask_BxSxS2_ik0 = jnp.where(jnp.broadcast_to(_validS2[:, None, :], (8, 128, 128)), 0, 1).astype(jnp.int32)
        mask_1x1xSxS2_ff0 = jnp.where(jnp.ones((1, 1, 128, 128), dtype=bool), 0.0, -1000000000.0).astype(jnp.float32)
        mask_SxS2_bk0 = jnp.logical_not(jnp.broadcast_to(_validS2[0:1, :], (128, 128)))
        _g = jax.random.normal(jax.random.fold_in(_rk, 9001), (2, 4), jnp.float32)
        _g = jnp.sign(_g) * jnp.maximum(jnp.abs(_g), 1.0) + (_g == 0) * 1.0
        g_xattn = _g[0]
        g_ffn = _g[1]
        return (x, ctx_4096, pos_BxS2, mask_BxSxS2_ik0, mask_1x1xSxS2_ff0, mask_SxS2_bk0, g_xattn, g_ffn)
    x, ctx_4096, pos_BxS2, mask_BxSxS2_ik0, mask_1x1xSxS2_ff0, mask_SxS2_bk0, g_xattn, g_ffn = _rec_inputs()

    def _L0_xattn_setup():
        import jax, jax.numpy as jnp
        import numpy as np
        B, S, E = (2, 256, 512)
        H, KVH, D = (32, 8, 128)
        GROUPS = H // KVH
        MAX_POS = 512
        ROPE_THETA = 10000.0

        def _rope_tables(max_pos, dim, theta):
            inv_freq = 1.0 / theta ** (jnp.arange(0, dim, 2, dtype=jnp.float32) / dim)
            t = jnp.arange(max_pos, dtype=jnp.float32)
            freqs = jnp.einsum('i,j->ij', t, inv_freq)
            emb = jnp.concatenate([freqs, freqs], axis=-1)
            return (jnp.cos(emb), jnp.sin(emb))

        def _rotate_half(x):
            x1, x2 = (x[..., :x.shape[-1] // 2], x[..., x.shape[-1] // 2:])
            return jnp.concatenate([-x2, x1], axis=-1)
        key = jax.random.key(seed)
        ks = jax.random.split(key, 8)
        scale_w = 1.0 / np.sqrt(E)
        query = jax.random.normal(ks[0], (B, S, E), dtype=jnp.float32)
        k_in = jax.random.normal(ks[1], (B, S, E), dtype=jnp.float32)
        v_in = jax.random.normal(ks[2], (B, S, E), dtype=jnp.float32)
        position_ids = jnp.broadcast_to(jnp.arange(S, dtype=jnp.int64), (B, S))
        src_mask = jnp.tril(jnp.ones((S, S), dtype=jnp.int32))
        src_mask = jnp.broadcast_to(src_mask, (B, S, S))
        Wq = jax.random.normal(ks[3], (E, H * D), dtype=jnp.float32) * scale_w
        Wk = jax.random.normal(ks[4], (E, KVH * D), dtype=jnp.float32) * scale_w
        Wv = jax.random.normal(ks[5], (E, KVH * D), dtype=jnp.float32) * scale_w
        Wo = jax.random.normal(ks[6], (H * D, E), dtype=jnp.float32) * scale_w
        return {'query': query, 'key': k_in, 'value': v_in, 'position_ids': position_ids, 'src_mask': src_mask, 'Wq': Wq, 'Wk': Wk, 'Wv': Wv, 'Wo': Wo}
    _L0_xattn_all = _L0_xattn_setup()
    _L0_xattn_in = {k: v for k, v in _L0_xattn_all.items() if k in ('Wq', 'Wk', 'Wv', 'Wo')}
    del _L0_xattn_all

    def _L0_ffn_setup():
        import jax, jax.numpy as jnp
        import numpy as np
        N_EXPERTS = 28
        TOP_K = 2
        RANK = 8
        LORA_ALPHA = 16
        SCALING = LORA_ALPHA / RANK
        TEMP = 1.0
        key = jax.random.key(seed)
        ks = jax.random.split(key, 5)
        B, S, D_IN, D_OUT = (4, 256, 512, 512)
        x = jax.random.normal(ks[0], (B, S, D_IN), dtype=jnp.float32)
        base_W = jax.random.normal(ks[1], (D_OUT, D_IN), dtype=jnp.float32) * (1.0 / np.sqrt(D_IN))
        gate_W = jax.random.normal(ks[2], (N_EXPERTS, D_IN), dtype=jnp.float32) * (1.0 / np.sqrt(D_IN))
        lora_A = jax.random.normal(ks[3], (N_EXPERTS, RANK, D_IN), dtype=jnp.float32) * (1.0 / np.sqrt(D_IN))
        lora_B = jax.random.normal(ks[4], (N_EXPERTS, D_OUT, RANK), dtype=jnp.float32) * 0.01
        return {'x': x, 'base_W': base_W, 'gate_W': gate_W, 'lora_A': lora_A, 'lora_B': lora_B}
    _L0_ffn_all = _L0_ffn_setup()
    _L0_ffn_in = {k: v for k, v in _L0_ffn_all.items() if k in ('base_W', 'gate_W', 'lora_A', 'lora_B')}
    del _L0_ffn_all

    def _L1_xattn_setup():
        import jax, jax.numpy as jnp
        import numpy as np
        NUM_HEADS = 32
        NUM_KV_HEADS = 8
        HEAD_DIM = 128
        HIDDEN = 512
        EPS = 1e-05

        def rmsnorm(x, w, eps=EPS):
            xf = x.astype(jnp.float32)
            var = jnp.mean(xf * xf, axis=-1, keepdims=True)
            return w * (xf * jax.lax.rsqrt(var + eps)).astype(x.dtype)
        key = jax.random.key(seed)
        ks = jax.random.split(key, 10)
        B, Q, KV = (1, 128, 6404)
        s = 1.0 / np.sqrt(HIDDEN)
        return {'hidden_states': jax.random.normal(ks[0], (B, Q, HIDDEN), jnp.float32), 'cross_attention_states': jax.random.normal(ks[1], (B, KV, HIDDEN), jnp.float32), 'attention_mask': jnp.zeros((B, 1, Q, KV), jnp.float32), 'q_proj_w': jax.random.normal(ks[2], (NUM_HEADS * HEAD_DIM, HIDDEN), jnp.float32) * s, 'k_proj_w': jax.random.normal(ks[3], (NUM_KV_HEADS * HEAD_DIM, HIDDEN), jnp.float32) * s, 'v_proj_w': jax.random.normal(ks[4], (NUM_KV_HEADS * HEAD_DIM, HIDDEN), jnp.float32) * s, 'o_proj_w': jax.random.normal(ks[5], (HIDDEN, NUM_HEADS * HEAD_DIM), jnp.float32) * s, 'q_norm_w': jnp.ones((HEAD_DIM,), jnp.float32), 'k_norm_w': jnp.ones((HEAD_DIM,), jnp.float32)}
    _L1_xattn_all = _L1_xattn_setup()
    _L1_xattn_in = {k: v for k, v in _L1_xattn_all.items() if k in ('q_proj_w', 'k_proj_w', 'v_proj_w', 'o_proj_w', 'q_norm_w', 'k_norm_w')}
    del _L1_xattn_all

    def _L1_ffn_setup():
        import jax, jax.numpy as jnp
        import numpy as np
        GROUP_SIZE = 32
        OUT_F, IN_F = (512, 512)
        key = jax.random.key(seed)
        k1, k2, k3, k4, k5 = jax.random.split(key, 5)
        x = jax.random.normal(k1, (4, 256, IN_F), dtype=jnp.float32)
        qweight = jax.random.randint(k2, (OUT_F, IN_F), 0, 32, dtype=jnp.int32)
        n_groups = OUT_F * IN_F // GROUP_SIZE
        scales = jax.random.uniform(k3, (n_groups, 1), dtype=jnp.float32, minval=0.0001, maxval=0.001)
        zeros = jax.random.randint(k4, (n_groups, 1), 0, 32).astype(jnp.float32)
        bias = jax.random.normal(k5, (OUT_F,), dtype=jnp.float32)
        return {'x': x, 'qweight': qweight, 'scales': scales, 'zeros': zeros, 'bias': bias}
    _L1_ffn_all = _L1_ffn_setup()
    _L1_ffn_in = {k: v for k, v in _L1_ffn_all.items() if k in ('qweight', 'scales', 'zeros', 'bias')}
    del _L1_ffn_all

    def _L2_xattn_setup():
        import jax, jax.numpy as jnp
        import numpy as np
        N_HEAD = 32
        D_MODEL = 512
        N_KV_GROUPS = 8
        D_HEAD = D_MODEL // N_HEAD
        H_PER_G = N_HEAD // N_KV_GROUPS
        KV_DIM = N_KV_GROUPS * D_HEAD
        B, S = (2, 256)
        key = jax.random.key(seed)
        ks = jax.random.split(key, 8)
        q = jax.random.normal(ks[0], (B, S, D_MODEL), dtype=jnp.float32)
        k = jax.random.normal(ks[1], (B, S, D_MODEL), dtype=jnp.float32)
        v = jax.random.normal(ks[2], (B, S, D_MODEL), dtype=jnp.float32)
        mask = jnp.tril(jnp.ones((S, S), dtype=bool))
        w_q = jax.random.uniform(ks[3], (D_MODEL, D_MODEL), dtype=jnp.float32) * 0.02
        w_k = jax.random.uniform(ks[4], (KV_DIM, D_MODEL), dtype=jnp.float32) * 0.02
        w_v = jax.random.uniform(ks[5], (KV_DIM, D_MODEL), dtype=jnp.float32) * 0.02
        w_out = jax.random.uniform(ks[6], (D_MODEL, D_MODEL), dtype=jnp.float32) * 0.02
        return {'q': q, 'k': k, 'v': v, 'w_q': w_q, 'w_k': w_k, 'w_v': w_v, 'w_out': w_out, 'mask': mask}
    _L2_xattn_all = _L2_xattn_setup()
    _L2_xattn_in = {k: v for k, v in _L2_xattn_all.items() if k in ('w_q', 'w_k', 'w_v', 'w_out')}
    del _L2_xattn_all

    def _L2_ffn_setup():
        import jax, jax.numpy as jnp
        import numpy as np
        HIDDEN = 512
        MOE_INTER = 128
        SHARED_INTER = 512
        NUM_EXPERTS = 16
        TOP_K = 2

        def _moe_forward(x, gate_w, w_gate_up, w_down, shared_w_gate_up, shared_w_down):
            orig_shape = x.shape
            x2 = x.reshape(-1, orig_shape[-1])
            gu_s = x2 @ shared_w_gate_up.T
            g_s, u_s = jnp.split(gu_s, 2, axis=-1)
            shared_out = jax.nn.silu(g_s) * u_s @ shared_w_down.T
            logits = x2 @ gate_w.T
            probs = jax.nn.softmax(logits, axis=-1)
            topk_vals, topk_idx = jax.lax.top_k(probs, TOP_K)
            topk_vals = topk_vals / jnp.sum(topk_vals, axis=-1, keepdims=True)
            combine = jnp.sum(jax.nn.one_hot(topk_idx, NUM_EXPERTS, dtype=x2.dtype) * topk_vals[..., None], axis=1)
            gu = jnp.einsum('th,eih->eti', x2, w_gate_up)
            g, u = jnp.split(gu, 2, axis=-1)
            act = jax.nn.silu(g) * u
            out_e = jnp.einsum('eti,ehi->eth', act, w_down)
            moe_out = jnp.einsum('eth,te->th', out_e, combine)
            return (moe_out + shared_out).reshape(orig_shape)
        key = jax.random.key(seed)
        ks = jax.random.split(key, 6)
        s = 0.02
        hidden_states = jax.random.normal(ks[0], (2, 256, HIDDEN), dtype=jnp.float32)
        gate_w = jax.random.normal(ks[1], (NUM_EXPERTS, HIDDEN), dtype=jnp.float32) * s
        w_gate_up = jax.random.normal(ks[2], (NUM_EXPERTS, 2 * MOE_INTER, HIDDEN), dtype=jnp.float32) * s
        w_down = jax.random.normal(ks[3], (NUM_EXPERTS, HIDDEN, MOE_INTER), dtype=jnp.float32) * s
        shared_w_gate_up = jax.random.normal(ks[4], (2 * SHARED_INTER, HIDDEN), dtype=jnp.float32) * s
        shared_w_down = jax.random.normal(ks[5], (HIDDEN, SHARED_INTER), dtype=jnp.float32) * s
        return {'hidden_states': hidden_states, 'gate_w': gate_w, 'w_gate_up': w_gate_up, 'w_down': w_down, 'shared_w_gate_up': shared_w_gate_up, 'shared_w_down': shared_w_down}
    _L2_ffn_all = _L2_ffn_setup()
    _L2_ffn_in = {k: v for k, v in _L2_ffn_all.items() if k in ('gate_w', 'w_gate_up', 'w_down', 'shared_w_gate_up', 'shared_w_down')}
    del _L2_ffn_all

    def _L3_xattn_setup():
        import jax, jax.numpy as jnp
        import numpy as np
        B, Q, K, D = (1, 128, 6404, 512)
        H, KVH, HD = (32, 8, 128)
        GROUPS = H // KVH
        EPS = 1e-05

        def _rmsnorm(x, w):
            xf = x.astype(jnp.float32)
            var = jnp.mean(xf * xf, axis=-1, keepdims=True)
            return (xf * jax.lax.rsqrt(var + EPS)).astype(x.dtype) * w
        key = jax.random.key(seed)
        ks = jax.random.split(key, 8)
        s = 0.02
        return {'hidden_states': jax.random.normal(ks[0], (B, Q, D), jnp.float32), 'cross_attention_states': jax.random.normal(ks[1], (B, K, D), jnp.float32), 'attention_mask': jnp.zeros((B, 1, Q, K), jnp.float32), 'Wq': jax.random.normal(ks[2], (H * HD, D), jnp.float32) * s, 'Wk': jax.random.normal(ks[3], (KVH * HD, D), jnp.float32) * s, 'Wv': jax.random.normal(ks[4], (KVH * HD, D), jnp.float32) * s, 'Wo': jax.random.normal(ks[5], (D, H * HD), jnp.float32) * s, 'q_norm_w': jnp.ones((HD,), jnp.float32), 'k_norm_w': jnp.ones((HD,), jnp.float32)}
    _L3_xattn_all = _L3_xattn_setup()
    _L3_xattn_in = {k: v for k, v in _L3_xattn_all.items() if k in ('Wq', 'Wk', 'Wv', 'Wo', 'q_norm_w', 'k_norm_w')}
    del _L3_xattn_all

    def _L3_ffn_setup():
        import jax, jax.numpy as jnp
        import numpy as np
        NUM_EXPERTS = 8
        D_IN = 512
        D_OUT = 512
        key = jax.random.key(seed)
        k_x, k_gw, k_gb, k_ew, k_eb = jax.random.split(key, 5)
        x = jax.random.normal(k_x, (4, 256, D_IN), dtype=jnp.float32)
        gate_w = jax.random.normal(k_gw, (NUM_EXPERTS, D_IN), dtype=jnp.float32) * 0.02
        gate_b = jax.random.normal(k_gb, (NUM_EXPERTS,), dtype=jnp.float32) * 0.02
        expert_w = jax.random.normal(k_ew, (NUM_EXPERTS, D_OUT, D_IN), dtype=jnp.float32) * 0.02
        expert_b = jax.random.normal(k_eb, (NUM_EXPERTS, D_OUT), dtype=jnp.float32) * 0.02
        return {'x': x, 'gate_w': gate_w, 'gate_b': gate_b, 'expert_w': expert_w, 'expert_b': expert_b}
    _L3_ffn_all = _L3_ffn_setup()
    _L3_ffn_in = {k: v for k, v in _L3_ffn_all.items() if k in ('gate_w', 'gate_b', 'expert_w', 'expert_b')}
    del _L3_ffn_all
    return {'x': x, 'ctx_4096': ctx_4096, 'pos_BxS2': pos_BxS2, 'mask_BxSxS2_ik0': mask_BxSxS2_ik0, 'mask_1x1xSxS2_ff0': mask_1x1xSxS2_ff0, 'mask_SxS2_bk0': mask_SxS2_bk0, 'g_xattn': g_xattn, 'g_ffn': g_ffn, 'L0_xattn_Wq': _L0_xattn_in['Wq'], 'L0_xattn_Wk': _L0_xattn_in['Wk'], 'L0_xattn_Wv': _L0_xattn_in['Wv'], 'L0_xattn_Wo': _L0_xattn_in['Wo'], 'L0_ffn_base_W': _L0_ffn_in['base_W'], 'L0_ffn_gate_W': _L0_ffn_in['gate_W'], 'L0_ffn_lora_A': _L0_ffn_in['lora_A'], 'L0_ffn_lora_B': _L0_ffn_in['lora_B'], 'L1_xattn_q_proj_w': _L1_xattn_in['q_proj_w'], 'L1_xattn_k_proj_w': _L1_xattn_in['k_proj_w'], 'L1_xattn_v_proj_w': _L1_xattn_in['v_proj_w'], 'L1_xattn_o_proj_w': _L1_xattn_in['o_proj_w'], 'L1_xattn_q_norm_w': _L1_xattn_in['q_norm_w'], 'L1_xattn_k_norm_w': _L1_xattn_in['k_norm_w'], 'L1_ffn_qweight': _L1_ffn_in['qweight'], 'L1_ffn_scales': _L1_ffn_in['scales'], 'L1_ffn_zeros': _L1_ffn_in['zeros'], 'L1_ffn_bias': _L1_ffn_in['bias'], 'L2_xattn_w_q': _L2_xattn_in['w_q'], 'L2_xattn_w_k': _L2_xattn_in['w_k'], 'L2_xattn_w_v': _L2_xattn_in['w_v'], 'L2_xattn_w_out': _L2_xattn_in['w_out'], 'L2_ffn_gate_w': _L2_ffn_in['gate_w'], 'L2_ffn_w_gate_up': _L2_ffn_in['w_gate_up'], 'L2_ffn_w_down': _L2_ffn_in['w_down'], 'L2_ffn_shared_w_gate_up': _L2_ffn_in['shared_w_gate_up'], 'L2_ffn_shared_w_down': _L2_ffn_in['shared_w_down'], 'L3_xattn_Wq': _L3_xattn_in['Wq'], 'L3_xattn_Wk': _L3_xattn_in['Wk'], 'L3_xattn_Wv': _L3_xattn_in['Wv'], 'L3_xattn_Wo': _L3_xattn_in['Wo'], 'L3_xattn_q_norm_w': _L3_xattn_in['q_norm_w'], 'L3_xattn_k_norm_w': _L3_xattn_in['k_norm_w'], 'L3_ffn_gate_w': _L3_ffn_in['gate_w'], 'L3_ffn_gate_b': _L3_ffn_in['gate_b'], 'L3_ffn_expert_w': _L3_ffn_in['expert_w'], 'L3_ffn_expert_b': _L3_ffn_in['expert_b']}

def reference(x, ctx_4096, pos_BxS2, mask_BxSxS2_ik0, mask_1x1xSxS2_ff0, mask_SxS2_bk0, g_xattn, g_ffn, L0_xattn_Wq, L0_xattn_Wk, L0_xattn_Wv, L0_xattn_Wo, L0_ffn_base_W, L0_ffn_gate_W, L0_ffn_lora_A, L0_ffn_lora_B, L1_xattn_q_proj_w, L1_xattn_k_proj_w, L1_xattn_v_proj_w, L1_xattn_o_proj_w, L1_xattn_q_norm_w, L1_xattn_k_norm_w, L1_ffn_qweight, L1_ffn_scales, L1_ffn_zeros, L1_ffn_bias, L2_xattn_w_q, L2_xattn_w_k, L2_xattn_w_v, L2_xattn_w_out, L2_ffn_gate_w, L2_ffn_w_gate_up, L2_ffn_w_down, L2_ffn_shared_w_gate_up, L2_ffn_shared_w_down, L3_xattn_Wq, L3_xattn_Wk, L3_xattn_Wv, L3_xattn_Wo, L3_xattn_q_norm_w, L3_xattn_k_norm_w, L3_ffn_gate_w, L3_ffn_gate_b, L3_ffn_expert_w, L3_ffn_expert_b):
    import jax
    import jax.numpy as jnp

    def _L0_xattn_ref(query, key, value, position_ids, src_mask, Wq, Wk, Wv, Wo):
        import jax, jax.numpy as jnp
        import numpy as np
        B, S, E = (2, 256, 512)
        H, KVH, D = (32, 8, 128)
        GROUPS = H // KVH
        MAX_POS = 512
        ROPE_THETA = 10000.0

        def _rope_tables(max_pos, dim, theta):
            inv_freq = 1.0 / theta ** (jnp.arange(0, dim, 2, dtype=jnp.float32) / dim)
            t = jnp.arange(max_pos, dtype=jnp.float32)
            freqs = jnp.einsum('i,j->ij', t, inv_freq)
            emb = jnp.concatenate([freqs, freqs], axis=-1)
            return (jnp.cos(emb), jnp.sin(emb))

        def _rotate_half(x):
            x1, x2 = (x[..., :x.shape[-1] // 2], x[..., x.shape[-1] // 2:])
            return jnp.concatenate([-x2, x1], axis=-1)
        nb, q_len, _ = query.shape
        q = (query @ Wq).reshape(nb, q_len, H, D).transpose(0, 2, 1, 3)
        k = (key @ Wk).reshape(nb, q_len, KVH, D).transpose(0, 2, 1, 3)
        v = (value @ Wv).reshape(nb, q_len, KVH, D).transpose(0, 2, 1, 3)
        cos_t, sin_t = _rope_tables(MAX_POS, D, ROPE_THETA)
        cos = cos_t[position_ids][:, None]
        sin = sin_t[position_ids][:, None]
        q = q * cos + _rotate_half(q) * sin
        k = k * cos + _rotate_half(k) * sin
        k = jnp.repeat(k, GROUPS, axis=1)
        v = jnp.repeat(v, GROUPS, axis=1)
        scores = jnp.einsum('bhqd,bhkd->bhqk', q, k) / jnp.sqrt(jnp.float32(D))
        mask = src_mask[:, None]
        scores = jnp.where(mask == 0, jnp.float32(-1000000000.0), scores)
        attn = jax.nn.softmax(scores, axis=-1)
        x = jnp.einsum('bhqk,bhkd->bhqd', attn, v)
        x = x.transpose(0, 2, 1, 3).reshape(nb, q_len, H * D)
        return x @ Wo

    def _L0_ffn_ref(x, base_W, gate_W, lora_A, lora_B):
        import jax, jax.numpy as jnp
        import numpy as np
        N_EXPERTS = 28
        TOP_K = 2
        RANK = 8
        LORA_ALPHA = 16
        SCALING = LORA_ALPHA / RANK
        TEMP = 1.0
        B, S, D_in = x.shape
        xf = x.reshape(B * S, D_in)
        base = xf @ base_W.T
        logits = xf @ gate_W.T
        top_vals, top_idx = jax.lax.top_k(logits, TOP_K)
        top_probs = jax.nn.softmax(top_vals / TEMP, axis=-1)
        N = xf.shape[0]
        gate_full = jnp.zeros((N, N_EXPERTS), dtype=xf.dtype).at[jnp.arange(N)[:, None], top_idx].add(top_probs)
        h = jnp.einsum('nd,erd->ner', xf, lora_A)
        h = h * (gate_full * SCALING)[:, :, None]
        lora_out = jnp.einsum('ner,eor->no', h, lora_B)
        out = base + lora_out
        return out.reshape(B, S, -1)

    def _L1_xattn_ref(hidden_states, cross_attention_states, attention_mask, q_proj_w, k_proj_w, v_proj_w, o_proj_w, q_norm_w, k_norm_w):
        import jax, jax.numpy as jnp
        import numpy as np
        NUM_HEADS = 32
        NUM_KV_HEADS = 8
        HEAD_DIM = 128
        HIDDEN = 512
        EPS = 1e-05

        def rmsnorm(x, w, eps=EPS):
            xf = x.astype(jnp.float32)
            var = jnp.mean(xf * xf, axis=-1, keepdims=True)
            return w * (xf * jax.lax.rsqrt(var + eps)).astype(x.dtype)
        B, Q, _ = hidden_states.shape
        KV = cross_attention_states.shape[1]
        n_rep = NUM_HEADS // NUM_KV_HEADS
        q = (hidden_states @ q_proj_w.T).reshape(B, Q, NUM_HEADS, HEAD_DIM).transpose(0, 2, 1, 3)
        k = (cross_attention_states @ k_proj_w.T).reshape(B, KV, NUM_KV_HEADS, HEAD_DIM).transpose(0, 2, 1, 3)
        v = (cross_attention_states @ v_proj_w.T).reshape(B, KV, NUM_KV_HEADS, HEAD_DIM).transpose(0, 2, 1, 3)
        q = rmsnorm(q, q_norm_w)
        k = jnp.repeat(k, n_rep, axis=1)
        v = jnp.repeat(v, n_rep, axis=1)
        k = rmsnorm(k, k_norm_w)
        scale = 1.0 / np.sqrt(HEAD_DIM)
        scores = jnp.einsum('bhqd,bhkd->bhqk', q, k) * scale + attention_mask
        attn = jax.nn.softmax(scores.astype(jnp.float32), axis=-1).astype(q.dtype)
        out = jnp.einsum('bhqk,bhkd->bhqd', attn, v)
        out = out.transpose(0, 2, 1, 3).reshape(B, Q, NUM_HEADS * HEAD_DIM)
        return out @ o_proj_w.T

    def _L1_ffn_ref(x, qweight, scales, zeros, bias):
        import jax, jax.numpy as jnp
        import numpy as np
        GROUP_SIZE = 32
        OUT_F, IN_F = (512, 512)
        w = qweight.astype(x.dtype).reshape(-1, GROUP_SIZE)
        w = (w - zeros) * scales
        w = w.reshape(OUT_F, IN_F)
        return jnp.einsum('bsi,oi->bso', x, w) + bias

    def _L2_xattn_ref(q, k, v, w_q, w_k, w_v, w_out, mask):
        import jax, jax.numpy as jnp
        import numpy as np
        N_HEAD = 32
        D_MODEL = 512
        N_KV_GROUPS = 8
        D_HEAD = D_MODEL // N_HEAD
        H_PER_G = N_HEAD // N_KV_GROUPS
        KV_DIM = N_KV_GROUPS * D_HEAD
        B, S = (2, 256)
        b, n, _ = q.shape
        s = k.shape[1]
        query = q @ w_q.T
        key = k @ w_k.T
        value = v @ w_v.T
        query = query.reshape(b, n, N_HEAD, D_HEAD).transpose(0, 2, 1, 3)
        query = query.reshape(b, N_KV_GROUPS, H_PER_G, n, D_HEAD)
        key = key.reshape(b, s, N_KV_GROUPS, D_HEAD).transpose(0, 2, 1, 3)
        value = value.reshape(b, s, N_KV_GROUPS, D_HEAD).transpose(0, 2, 1, 3)
        scores = jnp.einsum('bghnd,bgsd->bghns', query, key) / D_HEAD ** 0.5
        scores = jnp.where(mask, scores, jnp.finfo(scores.dtype).min)
        attention = jax.nn.softmax(scores, axis=-1)
        out = jnp.einsum('bghns,bgsd->bghnd', attention, value)
        out = out.transpose(0, 3, 1, 2, 4).reshape(b, n, D_MODEL)
        return out @ w_out.T

    def _L2_ffn_ref(hidden_states, gate_w, w_gate_up, w_down, shared_w_gate_up, shared_w_down):
        import jax, jax.numpy as jnp
        import numpy as np
        HIDDEN = 512
        MOE_INTER = 128
        SHARED_INTER = 512
        NUM_EXPERTS = 16
        TOP_K = 2

        def _moe_forward(x, gate_w, w_gate_up, w_down, shared_w_gate_up, shared_w_down):
            orig_shape = x.shape
            x2 = x.reshape(-1, orig_shape[-1])
            gu_s = x2 @ shared_w_gate_up.T
            g_s, u_s = jnp.split(gu_s, 2, axis=-1)
            shared_out = jax.nn.silu(g_s) * u_s @ shared_w_down.T
            logits = x2 @ gate_w.T
            probs = jax.nn.softmax(logits, axis=-1)
            topk_vals, topk_idx = jax.lax.top_k(probs, TOP_K)
            topk_vals = topk_vals / jnp.sum(topk_vals, axis=-1, keepdims=True)
            combine = jnp.sum(jax.nn.one_hot(topk_idx, NUM_EXPERTS, dtype=x2.dtype) * topk_vals[..., None], axis=1)
            gu = jnp.einsum('th,eih->eti', x2, w_gate_up)
            g, u = jnp.split(gu, 2, axis=-1)
            act = jax.nn.silu(g) * u
            out_e = jnp.einsum('eti,ehi->eth', act, w_down)
            moe_out = jnp.einsum('eth,te->th', out_e, combine)
            return (moe_out + shared_out).reshape(orig_shape)
        return _moe_forward(hidden_states, gate_w, w_gate_up, w_down, shared_w_gate_up, shared_w_down)

    def _L3_xattn_ref(hidden_states, cross_attention_states, attention_mask, Wq, Wk, Wv, Wo, q_norm_w, k_norm_w):
        import jax, jax.numpy as jnp
        import numpy as np
        B, Q, K, D = (1, 128, 6404, 512)
        H, KVH, HD = (32, 8, 128)
        GROUPS = H // KVH
        EPS = 1e-05

        def _rmsnorm(x, w):
            xf = x.astype(jnp.float32)
            var = jnp.mean(xf * xf, axis=-1, keepdims=True)
            return (xf * jax.lax.rsqrt(var + EPS)).astype(x.dtype) * w
        bsz, q_len, _ = hidden_states.shape
        kv_len = cross_attention_states.shape[1]
        q = (hidden_states @ Wq.T).reshape(bsz, q_len, H, HD).transpose(0, 2, 1, 3)
        k = (cross_attention_states @ Wk.T).reshape(bsz, kv_len, KVH, HD).transpose(0, 2, 1, 3)
        v = (cross_attention_states @ Wv.T).reshape(bsz, kv_len, KVH, HD).transpose(0, 2, 1, 3)
        q = _rmsnorm(q, q_norm_w)
        k = jnp.repeat(k, GROUPS, axis=1)
        v = jnp.repeat(v, GROUPS, axis=1)
        k = _rmsnorm(k, k_norm_w)
        scale = 1.0 / np.sqrt(HD)
        scores = jnp.einsum('bhqd,bhkd->bhqk', q, k) * scale
        scores = scores + attention_mask[:, :, :, :kv_len]
        probs = jax.nn.softmax(scores.astype(jnp.float32), axis=-1).astype(q.dtype)
        out = jnp.einsum('bhqk,bhkd->bhqd', probs, v)
        out = out.transpose(0, 2, 1, 3).reshape(bsz, q_len, H * HD)
        return out @ Wo.T

    def _L3_ffn_ref(x, gate_w, gate_b, expert_w, expert_b):
        import jax, jax.numpy as jnp
        import numpy as np
        NUM_EXPERTS = 8
        D_IN = 512
        D_OUT = 512
        orig_shape = x.shape
        xf = x.reshape(-1, x.shape[-1])
        gate_logits = xf @ gate_w.T + gate_b
        gates = jax.nn.softmax(gate_logits, axis=-1)
        selected = jnp.argmax(gates, axis=-1)
        out = jnp.zeros((xf.shape[0], expert_w.shape[1]), dtype=xf.dtype)
        for j in range(expert_w.shape[0]):
            yj = xf @ expert_w[j].T + expert_b[j]
            out = out + jnp.where((selected == j)[:, None], yj, 0.0)
        return out.reshape(*orig_shape[:-1], expert_w.shape[1])
    x = x + jnp.tanh(g_xattn[0]) * _L0_xattn_ref(_layernorm(x, axis=-1), ctx_4096, ctx_4096, pos_BxS2, mask_BxSxS2_ik0, L0_xattn_Wq, L0_xattn_Wk, L0_xattn_Wv, L0_xattn_Wo)
    x = x + jnp.tanh(g_ffn[0]) * _L0_ffn_ref(_layernorm(x, axis=-1), L0_ffn_base_W, L0_ffn_gate_W, L0_ffn_lora_A, L0_ffn_lora_B)
    x = x + jnp.tanh(g_xattn[1]) * _L1_xattn_ref(_layernorm(x, axis=-1), ctx_4096, mask_1x1xSxS2_ff0, L1_xattn_q_proj_w, L1_xattn_k_proj_w, L1_xattn_v_proj_w, L1_xattn_o_proj_w, L1_xattn_q_norm_w, L1_xattn_k_norm_w)
    x = x + jnp.tanh(g_ffn[1]) * _L1_ffn_ref(_layernorm(x, axis=-1), L1_ffn_qweight, L1_ffn_scales, L1_ffn_zeros, L1_ffn_bias)
    x = x + jnp.tanh(g_xattn[2]) * _L2_xattn_ref(_layernorm(x, axis=-1), ctx_4096, ctx_4096, L2_xattn_w_q, L2_xattn_w_k, L2_xattn_w_v, L2_xattn_w_out, mask_SxS2_bk0)
    x = x + jnp.tanh(g_ffn[2]) * _L2_ffn_ref(_layernorm(x, axis=-1), L2_ffn_gate_w, L2_ffn_w_gate_up, L2_ffn_w_down, L2_ffn_shared_w_gate_up, L2_ffn_shared_w_down)
    x = x + jnp.tanh(g_xattn[3]) * _L3_xattn_ref(_layernorm(x, axis=-1), ctx_4096, mask_1x1xSxS2_ff0, L3_xattn_Wq, L3_xattn_Wk, L3_xattn_Wv, L3_xattn_Wo, L3_xattn_q_norm_w, L3_xattn_k_norm_w)
    x = x + jnp.tanh(g_ffn[3]) * _L3_ffn_ref(_layernorm(x, axis=-1), L3_ffn_gate_w, L3_ffn_gate_b, L3_ffn_expert_w, L3_ffn_expert_b)
    return x

_drawn_inputs = setup_inputs


def setup_inputs(seed=0):
    import zlib

    import numpy as np

    out = dict(_drawn_inputs(seed))
    spreads = {'L1_xattn_q_norm_w': (1.0, 0.2),
     'L1_xattn_k_norm_w': (1.0, 0.2),
     'L3_xattn_q_norm_w': (1.0, 0.6),
     'L3_xattn_k_norm_w': (1.0, 0.6)}
    factors = {'L0_ffn_lora_A': 2.774,
     'L0_ffn_lora_B': 2.918,
     'L2_xattn_w_v': 3.805,
     'L2_xattn_w_out': 4.872,
     'L2_ffn_gate_w': 4.001,
     'L2_ffn_w_gate_up': 3.963,
     'L2_ffn_w_down': 4.178,
     'L3_ffn_expert_b': 26.036,
     'g_ffn': 21.792,
     'L2_ffn_shared_w_gate_up': 6.892,
     'L2_ffn_shared_w_down': 6.695,
     'L3_ffn_gate_b': 21.641,
     'L3_xattn_Wq': 8.0,
     'L3_xattn_Wk': 8.0,
     'L3_xattn_Wv': 4.859,
     'L3_xattn_Wo': 4.979,
     'L3_ffn_expert_w': 3.06}
    for name, (base, spread) in spreads.items():
        noise = np.random.default_rng([zlib.crc32(name.encode()), seed]).standard_normal(out[name].shape)
        drawn = base * np.exp(spread * noise) if base else spread * noise
        out[name] = jnp.asarray(drawn.astype(out[name].dtype))
    for name, factor in factors.items():
        out[name] = (out[name] * factor).astype(out[name].dtype)
    return out
```

```python
from collections import defaultdict
from contextlib import ExitStack

import numpy as np
import concourse.bass as bass
from concourse import mybir

F32 = mybir.dt.float32
F32R = mybir.dt.float32r
I32 = mybir.dt.int32
U8 = mybir.dt.uint8
I8 = mybir.dt.int8
ALU = mybir.AluOpType
ACT = mybir.ActivationFunctionType
AX = mybir.AxisListType.X

P = 128
NB = 8
T = NB * P
D = 512
CH = D // P
G = 8
R = 4
HG = R * P
PIECE = 1024
SLOTS = 8
EPS = 1e-5
MASKED = -1e9
FMIN = float(np.finfo(np.float32).min)
MAX_POS, THETA = 512, 10000.0
E0, RANK, LORA_SCALE = 28, 8, 2.0
E2, SHARED_TILES = 16, 4
E3 = 8
HL = E0 * RANK
VSLOTS = 6
LAG_B, LAG_C, LAG_D, LAG_E, LAG_F = 1, 2, 4, 5, 6
FAR = -3.0e38


class Queues:

    def __init__(self, new_semaphore):
        self.new_semaphore = new_semaphore
        self.sems, self.count = {}, defaultdict(int)
        self.items = {e: [] for e in ("sync", "act", "dve", "pool", "pe")}
        self.passed = {e: {} for e in self.items}

    def put(self, engine, issue, after=(), done=None, by=1):
        for token in after:
            if token is None:
                continue
            name, value = token
            if self.passed[engine].get(name, 0) < value:
                self.passed[engine][name] = value
                self.items[engine].append((None, name, value))
        if done is not None:
            done = f"{engine}_{done}"
            if done not in self.sems:
                self.sems[done] = self.new_semaphore(done)
            self.count[done] += by
        self.items[engine].append((issue, done, by))
        return (done, self.count[done]) if done else None

    def wait_all(self, engine, prefixes):
        for name, value in self.count.items():
            if name.startswith(prefixes):
                self.items[engine].append((None, name, value))

    def emit(self, engine, eng):
        for issue, name, n in self.items[engine]:
            if issue is None:
                eng.wait_ge(self.sems[name], n)
            else:
                ins = issue(eng)
                if name is not None:
                    ins.then_inc(self.sems[name], n)


def build(nc, io, out, sublayers=8):
    with ExitStack() as ctx:
        def sb(name, shape, dt=F32):
            return ctx.enter_context(nc.sbuf_tensor(name, shape, dt))

        def pb(name, width):
            return ctx.enter_context(nc.psum_tensor(name, [P, width], F32))

        def new_semaphore(name):
            return ctx.enter_context(nc.semaphore(name))

        qs = Queues(new_semaphore)
        put = qs.put

        X = sb("X", [P, NB, D])
        xnT = [sb(f"xnT_{k}", [P, CH, T], F32R) for k in "hl"]
        ctxT = [sb(f"ctxT_{k}", [P, CH, T], F32R) for k in "hl"]
        ring = [sb(f"ring_{k}", [P, SLOTS, PIECE], F32R) for k in "hl"]
        raw = [sb(f"raw_{k}", [P, PIECE]) for k in range(2)]
        qk = sb("qk", [P, (R + 1) * P])
        sq = sb("sq", [P, (R + 1) * P])
        qT = [sb(f"qT_{k}", [P, HG], F32R) for k in "hl"]
        kT = [sb(f"kT_{k}", [P, P], F32R) for k in "hl"]
        v = [sb(f"v_{k}", [P, VSLOTS, P], F32R) for k in "hl"]
        spare = [sb(f"spare_{k}", [P, 2 * P], F32R) for k in "hl"]
        hsT = [m[0:HL // 2, :] for m in spare]
        vall = [m[:, 0:P] for m in spare]
        S = sb("S", [P, 2, HG])
        W = sb("W", [P, 2, HG])
        pT = [sb(f"pT_{k}", [P, HG], F32R) for k in "hl"]
        oT = [sb(f"oT_{k}", [P, HG], F32R) for k in "hl"]
        tables = sb("tables", [P, NB, 2 * P])
        mask0 = [sb("mask0_keep", [P, NB, P], I8), sb("mask0_minus", [P, NB, P], I8)]
        mask13 = sb("mask13", [P, P])
        mask2u = sb("mask2u", [P, P], U8)
        mask2 = tables[:, NB // 2, 0:P]
        ident = sb("ident", [P, P])
        xn = sb("xn", [P, D])
        routers = [sb(f"routers_{k}", [P, CH * (E2 + E3)], F32R) for k in "hl"]
        bias = [sb(f"bias_{k}", [E3 + 1, D], F32R) for k in "hl"]
        last_row = sb("last_row", [E3 + 1, P], F32R)
        onehotT = spare[0][0:E3, P:2 * P]
        gates = sb("gates", [P, 8])
        comb = sb("comb", [P, NB, E2])
        pos = sb("pos", [P, NB], I32)
        norm_w = sb("norm_w", [P, 4])
        wqk = sb("wqk", [P, 2])
        groupmask = sb("groupmask", [P, G])
        gate_b = sb("gate_b", [P, E3])
        rev = sb("rev", [P, E0])
        pw = sb("pw", [P, 8])
        st6 = sb("st6", [P, 6])
        mv = sb("mv", [P, 2])
        rstd = sb("rstd", [P, 2])
        ss = sb("ss", [P, 8])
        rn = sb("rn", [P, 2, 8])
        nmx = sb("nmx", [P, 2, R])
        den = sb("den", [P, 2, R])
        rden = sb("rden", [P, 2, R])
        rt = sb("rt", [P, 8, E0])
        r1 = sb("r1", [P, 16])
        hs = sb("hs", [P, HL])

        B_qkv = pb("B_qkv", 1024)
        B_qkT = pb("B_qkT", 1024)
        B_sc = pb("B_sc", 512)
        B_pt = pb("B_pt", 512)
        B_oT = pb("B_oT", 512)
        B_out = pb("B_out", 512)
        free = defaultdict(list)

        def f32(ap):
            return ap.bitcast(F32)

        def act_copy(dst, src, scale=1.0):
            return lambda e: e.activation(dst, src, ACT.Copy, scale=scale)

        def sub(dst, a, b):
            return lambda e: e.tensor_tensor(dst, a, b, ALU.subtract)

        def split(bank, hi, lo, after, name, scale=1.0):
            h = put("act", act_copy(hi, bank, scale), after, f"{name}_hi")
            if isinstance(scale, float):
                return put("dve", sub(lo, bank, f32(hi)), [h], f"{name}_lo")
            return put("dve", lambda e: e.scalar_tensor_tensor(out=lo, in0=bank, scalar=scale, in1=f32(hi),
                                                               op0=ALU.mult, op1=ALU.subtract), [h], f"{name}_lo")

        def products(dst, pairs, after, done=None, more=()):
            steps = []
            for (ah, al), (bh, bl) in pairs:
                steps += [(ah, bh), (ah, bl), (al, bh)]
            steps += more
            token = None
            for n, (a, b) in enumerate(steps):
                token = put("pe", lambda e, a=a, b=b, n=n: e.matmul(dst, a, b, start=n == 0, stop=n == len(steps) - 1),
                            after if n == 0 else (), done if n == len(steps) - 1 else None)
            return token

        raw_free = [None, None]
        loads = [0]

        def load(src, width=PIECE, rows=P, dst_dt=None):
            k = loads[0] % 2
            loads[0] += 1
            dst = raw[k][0:rows, 0:width]
            if dst_dt is not None:
                dst = dst.bitcast(dst_dt)
            return k, put("sync", lambda e: e.dma_start(dst, src), [raw_free[k]], f"raw{k}", 16)

        def split_raw(k, hi, lo, landed, width=PIECE, after=()):
            src = raw[k][:, 0:width]
            if len(hi.shape) == 3:
                src = src.rearrange("p (a n) -> p a n", a=hi.shape[1])
            h = put("act", act_copy(hi, src), [landed, *after], "piece_hi")
            raw_free[k] = put("pool", sub(lo, src, f32(hi)), [h], "piece_lo")
            return raw_free[k]

        plan = []
        held = []
        slot_free = [(s, None, -1) for s in range(SLOTS)]

        def piece(n):
            assert n < len(held), f"piece {n} is used before its turn: {len(held)} are in"
            slot, token = held[n]
            return (ring[0][:, slot, :], ring[1][:, slot, :]), token

        def release(n, token, now):
            slot_free.append((held[n][0], token, now))

        def advance(now, most):
            while most and len(held) < len(plan) and slot_free and slot_free[0][2] < now:
                slot, released, _ = slot_free.pop(0)
                hi, lo = ring[0][:, slot, :], ring[1][:, slot, :]
                kind, at = plan[len(held)]
                if kind == "float":
                    k, landed = load(io["pieces"][at])
                    token = split_raw(k, hi, lo, landed, after=[released])
                else:
                    k, landed = load(io["quant"][at], dst_dt=I32)
                    kz, zlanded = load(io["zeros"][at])
                    w = put("dve", lambda e, k=k, kz=kz: e.tensor_tensor(raw[k][:, :], raw[k][:, :].bitcast(I32),
                                                                         raw[kz][:, :], ALU.subtract),
                            [landed, zlanded], "dequant")
                    raw_free[k] = raw_free[kz] = w
                    loads[0] += 1
                    ksc, slanded = load(io["scales"][at])
                    assert ksc == kz
                    w = put("dve", lambda e, k=k, kz=kz: e.tensor_tensor(raw[k][:, :], raw[k][:, :], raw[kz][:, :],
                                                                         ALU.mult), [slanded, w], "dequant")
                    raw_free[kz] = w
                    token = split_raw(k, hi, lo, w, after=[released])
                held.append((slot, token))
                most -= 1

        small = [0]

        def small_load(dst, src, after=()):
            small[0] += 1
            return put("act", lambda e: e.dma_start(dst, src), after, f"small{small[0]}", 16)

        def rows(vec, n=P):
            return vec.partition_broadcast(n)

        x_ready = [small_load(X[:, b, :], io["x"][b]) for b in range(NB)]
        t_ident = small_load(ident[:, :], io["ident"])
        t_gates = [small_load(gates[:, 0:4], rows(io["g_xattn"])), small_load(gates[:, 4:8], rows(io["g_ffn"]))]
        t_pos = small_load(pos[:, :], io["pos"])
        t_m0 = small_load(S[:, :, :].rearrange("p s n -> p (s n)").bitcast(I32), io["mask0"])
        t_m13 = small_load(mask13[:, :], io["mask13"])
        t_m2 = small_load(mask2u[:, :].bitcast(I32), io["mask2"])
        t_nw = [small_load(norm_w[:, n:n + 1], io["norm_w"][n]) for n in range(4)]
        t_gm = small_load(groupmask[:, :], io["groupmask"])
        t_gate_b = small_load(gate_b[:, :], rows(io["gate_b"]))
        t_rev = small_load(rev[:, :], rows(io["rev"]))
        biases = W[0:E3 + 1, 0, :]
        t_bias = small_load(biases, io["bias"])
        t_last_row = small_load(W[0:E3 + 1, 1, 0:P], io["last_row"])
        t_tanh = put("act", lambda e: e.activation(gates[:, :], gates[:, :], ACT.Tanh), t_gates, "tanh_gates")
        t_pw = put("pool", lambda e: e.memset(pw[:, :], -0.5), (), "const")
        t = put("dve", lambda e: e.tensor_scalar(mask0[0][:, :, :], S[:, :, :].rearrange("p s (b k) -> p (s b) k", k=P)
                                                 .bitcast(I32), 0.0, None, ALU.not_equal), [t_m0], "const")
        free["S0"] = free["S1"] = [t]
        t_mask0 = put("dve", lambda e: e.tensor_scalar(mask0[1][:, :, :], mask0[0][:, :, :], -1.0, None, ALU.add),
                      [t], "const")
        t_wqk = put("dve", lambda e: e.tensor_tensor(wqk[:, :], norm_w[:, 0:2], norm_w[:, 2:4], ALU.mult), t_nw, "const")
        t = put("dve", lambda e: e.tensor_copy(bias[0][:, :], biases), [t_bias], "const")
        put("dve", lambda e: e.tensor_copy(last_row[:, :], W[0:E3 + 1, 1, 0:P]), [t_last_row])
        t_biases = put("dve", sub(bias[1][:, :], biases, f32(bias[0][:, :])), [t], "const")
        free["W0"] = free["W1"] = [t_biases]
        t_rope = []
        for b in range(NB):
            t_rope.append(put("pool", lambda e, b=b: e.indirect_dma_start(
                out=tables[:, b, :], out_offset=None, in_=io["rope"],
                in_offset=bass.IndirectOffsetOnAxis(ap=pos[:, b:b + 1], axis=0)), [t_pos], f"rope{b}", 16))
        for c in range(CH):
            k, landed = load(io["ctxT"][c])
            t_ctx = split_raw(k, ctxT[0][:, c, :], ctxT[1][:, c, :], landed)
        k, landed = load(io["routers"], CH * (E2 + E3))
        t_routers = split_raw(k, routers[0][:, :], routers[1][:, :], landed, CH * (E2 + E3))

        x_done = list(x_ready)
        xnT_free = [None] * NB
        xnT_ready = [None] * NB
        xn_ready = [None] * NB

        def ln_stats(b):
            t = put("dve", lambda e: e.bn_stats(st6[:, :], X[:, b, :]), [x_done[b], *free["st6"]], "ln")
            t = put("dve", lambda e: e.bn_aggr(mv[:, :], st6[:, :]), [t, *free["mv"]], "ln")
            t2 = put("pool", lambda e: e.tensor_scalar(rstd[:, 0:1], mv[:, 1:2], EPS, 1.0, ALU.add, ALU.mult), [t], "ln")
            t2 = put("pool", lambda e: e.tensor_tensor(rstd[:, 1:2], rstd[:, 0:1], pw[:, 0:1], ALU.pow), [t2, t_pw], "ln")
            t = put("dve", lambda e: e.tensor_scalar(xn[:, :], X[:, b, :], mv[:, 0:1], rstd[:, 1:2],
                                                     ALU.subtract, ALU.mult), [t2, *free["xn"]], "ln")
            free["mv"] = [t]
            xn_ready[b] = t

        def ln_turn(b):
            for c in range(CH):
                t = put("pe", lambda e, c=c: e.transpose(B_pt[:, c * P:(c + 1) * P], xn[:, c * P:(c + 1) * P], ident[:, :]),
                        [xn_ready[b], t_ident, *free["B_pt"]] if c == 0 else (), "ln_turn" if c == CH - 1 else None)
            free["xn"] = [t]
            cols = slice(b * P, (b + 1) * P)
            bank = B_pt[:, :].rearrange("p (c t) -> p c t", c=CH)
            t = split(bank, xnT[0][:, :, cols], xnT[1][:, :, cols], [t, *([xnT_free[b]] if xnT_free[b] else [])], "xnT")
            free["B_pt"] = [t]
            xnT_ready[b] = t

        def xn_cols(c, b):
            return tuple(m[:, c, b * P:(b + 1) * P] for m in xnT)

        def ctx_cols(c, b):
            return tuple(m[:, c, b * P:(b + 1) * P] for m in ctxT)

        events = defaultdict(list)

        def at(iteration, order, what, *args):
            events[iteration].append((order, len(events[iteration]), what, args))

        def attention(layer, first, base):
            kind = ("rope", "norm", "plain", "norm")[layer]
            scale = 0.25 if kind == "plain" else float(P) ** -0.5
            gate = gates[:, layer:layer + 1]
            small_heads = kind == "plain"
            units = [(g, b) for g in range(G) for b in range(NB)] if not small_heads else \
                    [(g, b) for b in range(NB) for g in range(G)]
            state = [dict() for _ in units]
            k_scale = wqk[:, layer // 2:layer // 2 + 1] if kind == "norm" else 1.0
            tokens = {}

            def fill_tables():
                tokens["mask2"] = put("dve", lambda e: e.tensor_scalar(mask2, mask2u[:, :], -1.0, -FMIN, ALU.add, ALU.mult),
                                      [t_m2, *free["tables"]], "mask2")
                tokens["cols"] = put("sync", lambda e: e.dma_start(tables[:, 0:4, :], rows(io["groupcols"])),
                                     free["tables"], "groupcols", 16)

            if small_heads:
                at(first - 1, 90, fill_tables)

            def pieces_of(g):
                return base if small_heads else base + 5 * g

            def stage_a(u, now):
                g, b = units[u]
                s = state[u]
                vs = u % VSLOTS
                if not small_heads or g == 0:
                    n = pieces_of(g)
                    (q0, tq0), (q1, tq1), (kv, tkv) = piece(n), piece(n + 1), piece(n + 2)
                    wq = [tuple(m[:, (c % 2) * HG:(c % 2 + 1) * HG] for m in (q0, q1)[c // 2]) for c in range(CH)]
                    wkv = [tuple(m[:, c * 2 * P:(c + 1) * 2 * P] for m in kv) for c in range(CH)]
                    products(B_qkv[:, 0:HG], [(xn_cols(c, b), wq[c]) for c in range(CH)],
                             [xnT_ready[b], tq0, tq1, *free["B_qkv"]])
                    t = products(B_qkv[:, HG:HG + 2 * P], [(ctx_cols(c, b), wkv[c]) for c in range(CH)], [t_ctx, tkv], "qkv")
                    xnT_free[b] = t
                    if b == NB - 1:
                        for m in range(3):
                            release(n + m, t, now)
                    vbank = B_qkv[:, HG + P:HG + 2 * P]
                    bank = B_qkv[:, 0:HG + P].rearrange("p (h d) -> p h d", d=P)
                    qk3 = qk[:, :].rearrange("p (h d) -> p h d", d=P)
                    sq3 = sq[:, :].rearrange("p (h d) -> p h d", d=P)
                    vdst = [m[:, :] for m in vall] if small_heads else [m[:, vs, :] for m in v]
                    if kind == "norm":
                        t_sq = put("act", lambda e: e.activation(sq[:, :], B_qkv[:, 0:HG + P], ACT.Square),
                                   [t, *free["sq"]], "squares")
                    if kind == "plain":
                        s["qk"] = put("act", act_copy(qk[:, :], B_qkv[:, 0:HG + P]), [t, *free["qk"]], "qk_copy")
                    t_v = split(vbank, vdst[0], vdst[1], [t, *(free["spare"] if small_heads else free[f"v{vs}"])], "v")
                    if kind == "norm":
                        t = put("dve", lambda e: e.tensor_reduce(ss[:, 0:R + 1], sq3, AX, ALU.add),
                                [t_sq, *free["ss"]], "sumsq")
                        free["sq"] = [t]
                        r = u % 2
                        t = put("pool", lambda e: e.tensor_scalar(rn[:, r, 0:R + 1], ss[:, 0:R + 1], 1.0 / P, EPS,
                                                                  ALU.mult, ALU.add), [t, *free[f"rn{r}"]], "rms")
                        free["ss"] = [t]
                        s["rn"] = put("pool", lambda e: e.tensor_tensor(rn[:, r, 0:R + 1], rn[:, r, 0:R + 1],
                                                                        pw[:, 0:R + 1], ALU.pow), [t, t_pw], "rms")
                    elif kind == "rope":
                        cos = tables[:, b, 0:P].unsqueeze(1).to_broadcast([P, R + 1, P])
                        half = P // 2
                        sin = tables[:, b, P:2 * P].unsqueeze(1).to_broadcast([P, R + 1, P])
                        t1 = put("dve", lambda e: e.tensor_tensor(sq3, bank, cos, ALU.mult),
                                 [t_v, t_rope[b], *free["sq"]], "rope")
                        put("dve", lambda e: e.tensor_tensor(qk3[:, :, 0:half], bank[:, :, half:P], sin[:, :, 0:half],
                                                             ALU.mult), free["qk"])
                        t = put("dve", lambda e: e.tensor_tensor(qk3[:, :, half:P], bank[:, :, 0:half], sin[:, :, half:P],
                                                                 ALU.mult), (), "rope")
                        free["B_qkv"] = [t]
                        free["tables"] = [t]
                        s["qk"] = put("pool", lambda e: e.tensor_tensor(qk[:, :], qk[:, :], sq[:, :], ALU.add), [t], "rope")
                        free["sq"] = [s["qk"]]
                    else:
                        free["B_qkv"] = [t_v]
                    s["v"] = t_v
                    if small_heads:
                        for uu in range(u, u + G):
                            state[uu]["vall"] = t_v
                if small_heads:
                    cols = tables[:, 0:4, :].rearrange("p a (c n) -> p (a c) n", n=P)[:, g, :]
                    for m in range(2):
                        t = put("pool", lambda e, m=m: e.tensor_tensor(v[m][:, vs, :], f32(vall[m][:, :]), cols, ALU.mult),
                                [s["vall"], tokens["cols"], *free[f"v{vs}"]], "v_group")
                    s["v"] = t
                    if g == G - 1:
                        free["spare"] = [t]

            def stage_a2(u):
                s = state[u]
                bank = B_qkv[:, 0:HG + P].rearrange("p (h d) -> p h d", d=P)
                r = u % 2
                s["qk"] = put("dve", lambda e: e.tensor_tensor(
                    qk[:, :].rearrange("p (h d) -> p h d", d=P), bank,
                    rn[:, r, 0:R + 1].unsqueeze(2).to_broadcast([P, R + 1, P]), ALU.mult),
                    [s["rn"], s["v"], *free["qk"]], "qk_norm")
                free["B_qkv"] = free[f"rn{r}"] = [s["qk"]]

            def stage_b(u):
                g, b = units[u]
                s = state[u]
                if not small_heads or g == 0:
                    for h in range(R + 1):
                        t = put("pe", lambda e, h=h: e.transpose(B_qkT[:, h * P:(h + 1) * P], qk[:, h * P:(h + 1) * P],
                                                                 ident[:, :]),
                                [s["qk"], *free["B_qkT"]] if h == 0 else (), "qk_turn" if h == R else None)
                    free["qk"] = [t]
                    s["qT"] = split(B_qkT[:, 0:HG], qT[0][:, :], qT[1][:, :], [t, *free["qT"]], "qT")
                    for uu in range(u, u + G if small_heads else u + 1):
                        state[uu]["turned"], state[uu]["qT"] = t, s["qT"]
                ks = groupmask[:, g:g + 1] if small_heads else k_scale
                s["kT"] = split(B_qkT[:, HG:HG + P], kT[0][:, :], kT[1][:, :],
                                [s["turned"], t_gm, t_wqk, *free["qT"]], "kT", ks)
                free["B_qkT"] = [s["kT"]]

            def stage_c(u):
                g, b = units[u]
                s = state[u]
                k = u % 2
                for r in range(R):
                    cols = slice(r * P, (r + 1) * P)
                    t = products(B_sc[:, cols], [((qT[0][:, cols], qT[1][:, cols]), (kT[0][:, :], kT[1][:, :]))],
                                 [s["qT"], s["kT"], *free["B_sc"]], "scores" if r == R - 1 else None)
                free["qT"] = [t]
                bank = B_sc[:, :].rearrange("p (r k) -> p r k", r=R)
                S3 = S[:, k, :].rearrange("p (r k) -> p r k", r=R)

                def per_head(m):
                    return m.unsqueeze(1).to_broadcast([P, R, P])

                if kind == "rope":
                    keep, minus = per_head(mask0[0][:, b, :]), per_head(mask0[1][:, b, :])
                    t = put("dve", lambda e: e.scalar_tensor_tensor(out=S3, in0=bank, scalar=scale, in1=keep, op0=ALU.mult,
                                                                    op1=ALU.mult), [t, t_mask0, *free[f"S{k}"]], "mask")
                    free["B_sc"] = [t]
                    t = put("dve", lambda e: e.scalar_tensor_tensor(out=S3, in0=minus, scalar=-MASKED, in1=S3, op0=ALU.mult,
                                                                    op1=ALU.add), [t], "mask")
                else:
                    m = per_head(mask2 if small_heads else mask13[:, :])
                    t = put("dve", lambda e: e.scalar_tensor_tensor(out=S3, in0=bank, scalar=scale, in1=m, op0=ALU.mult,
                                                                    op1=ALU.add), [t, tokens["mask2"] if small_heads else t_m13, *free[f"S{k}"]], "mask")
                    free["B_sc"] = [t]
                s["nmx"] = put("dve", lambda e: e.tensor_reduce(nmx[:, k, :], S3, AX, ALU.max, negate=True), [t], "max")

            def stage_c_exp(u):
                s = state[u]
                k = u % 2
                for r in range(R):
                    cols = slice(r * P, (r + 1) * P)
                    t = put("act", lambda e, r=r, cols=cols: e.activation(W[:, k, cols], S[:, k, cols], ACT.Exp,
                                                                         bias=nmx[:, k, r:r + 1],
                                                                         accum_out=den[:, k, r:r + 1]),
                            [s["nmx"], *free[f"W{k}"]] if r == 0 else (), "exp" if r == R - 1 else None)
                free[f"S{k}"] = [t]
                s["exp"] = t

            def stage_c_norm(u):
                s = state[u]
                k = u % 2
                t = put("dve", lambda e: e.reciprocal(rden[:, k, :], den[:, k, :]), [s["exp"]], "rden")
                W3 = W[:, k, :].rearrange("p (r k) -> p r k", r=R)
                s["p"] = put("pool", lambda e: e.tensor_tensor(W3, W3, rden[:, k, :].unsqueeze(2).to_broadcast([P, R, P]),
                                                               ALU.mult), [t], "probs")

            def stage_d(u):
                s = state[u]
                k = u % 2
                for r in range(R):
                    cols = slice(r * P, (r + 1) * P)
                    t = put("pe", lambda e, cols=cols: e.transpose(B_pt[:, cols], W[:, k, cols], ident[:, :]),
                            [s["p"], *free["B_pt"]] if r == 0 else (), "p_turn" if r == R - 1 else None)
                free[f"W{k}"] = [t]
                s["pT"] = split(B_pt[:, :], pT[0][:, :], pT[1][:, :], [t, *free["pT"]], "pT")
                free["B_pt"] = [s["pT"]]

            def stage_e(u):
                g, b = units[u]
                s = state[u]
                vs = u % VSLOTS
                begin, end = (g == 0, g == G - 1) if small_heads else (True, True)
                steps = [(v[0], pT[0]), (v[0], pT[1]), (v[1], pT[0])]
                for n, (a, c) in enumerate(steps):
                    t = put("pe", lambda e, a=a, c=c, n=n: e.matmul(B_oT[:, :], a[:, vs, :], c[:, :], start=begin and n == 0,
                                                                    stop=end and n == 2),
                            [s["pT"], s["v"], *(free["B_oT"] if begin else ())] if n == 0 else (), "pv" if n == 2 else None)
                free["pT"] = [t]
                free[f"v{vs}"] = [t]
                if end:
                    s["oT"] = split(B_oT[:, :], oT[0][:, :], oT[1][:, :], [t, *free["oT"]], "oT")
                    free["B_oT"] = [s["oT"]]

            def stage_f(u, now):
                g, b = units[u]
                if small_heads and g != G - 1:
                    return
                n = pieces_of(g) + 3
                (w0, tw0), (w1, tw1) = piece(n), piece(n + 1)
                pairs = [(tuple(m[:, r * P:(r + 1) * P] for m in oT),
                          tuple(m[:, (r % 2) * D:(r % 2 + 1) * D] for m in (w0, w1)[r // 2])) for r in range(R)]
                t = products(B_out[:, :], pairs, [state[u]["oT"], tw0, tw1, *free["B_out"]], "attn_out")
                free["oT"] = [t]
                if b == NB - 1:
                    release(n, t, now)
                    release(n + 1, t, now)
                add_to_x(b, B_out, "B_out", gate, t)

            for u in range(len(units)):
                i = first + u
                at(i, 70, stage_a, u, i)
                if kind == "norm":
                    at(i + 1, 10, stage_a2, u)
                at(i + LAG_B, 50, stage_b, u)
                at(i + LAG_C, 40, stage_c, u)
                at(i + LAG_C, 60, stage_c_exp, u)
                at(i + LAG_C, 80, stage_c_norm, u)
                at(i + LAG_D, 30, stage_d, u)
                at(i + LAG_E, 20, stage_e, u)
                at(i + LAG_F, 0, stage_f, u, i + LAG_F)
            if small_heads:
                return [first + b * G + G - 1 + LAG_F for b in range(NB)]
            return [first + (G - 1) * NB + b + LAG_F for b in range(NB)]

        def add_to_x(b, bank, bank_name, factor, token, after=()):
            t = put("dve", lambda e: e.scalar_tensor_tensor(out=X[:, b, :], in0=bank[:, :], scalar=factor, in1=X[:, b, :],
                                                            op0=ALU.mult, op1=ALU.add),
                    [token, x_done[b], t_tanh, *after], "x_add")
            free[bank_name] = [t]
            x_done[b] = t

        rt_done = [None]

        def chain(issue, *after):
            rt_done[0] = put("dve", issue, [rt_done[0], *after], "route")
            return rt_done[0]

        def first_max(onehot, top, src, n):
            chain(lambda e: e.tensor_reduce(top, src, AX, ALU.max))
            chain(lambda e: e.scalar_tensor_tensor(out=rt[:, 6, 0:n], in0=src, scalar=top, in1=rev[:, 0:n],
                                                   op0=ALU.is_equal, op1=ALU.mult), t_rev)
            chain(lambda e: e.tensor_reduce(r1[:, 15:16], rt[:, 6, 0:n], AX, ALU.max))
            chain(lambda e: e.tensor_scalar(onehot, rt[:, 6, 0:n], r1[:, 15:16], None, ALU.is_equal))

        def second_max(onehot2, top2, onehot1, src, n):
            chain(lambda e: e.scalar_tensor_tensor(out=rt[:, 5, 0:n], in0=onehot1, scalar=FAR, in1=src,
                                                   op0=ALU.mult, op1=ALU.add))
            first_max(onehot2, top2, rt[:, 5, 0:n], n)

        def softmax_rows(dst, bank, n, token):
            t = chain(lambda e: e.tensor_reduce(r1[:, 0:1], bank, AX, ALU.max, negate=True), token)
            t = put("act", lambda e: e.activation(rt[:, 0, 0:n], bank, ACT.Exp, bias=r1[:, 0:1], accum_out=r1[:, 1:2]),
                    [t], "route_exp")
            chain(lambda e: e.reciprocal(r1[:, 2:3], r1[:, 1:2]), t)
            chain(lambda e: e.tensor_scalar(dst, rt[:, 0, 0:n], r1[:, 2:3], None, ALU.mult))
            return t

        def router_logits(b, first_col, n):
            def w(c):
                return tuple(m[:, CH * first_col + c * n:CH * first_col + (c + 1) * n] for m in routers)
            return products(B_sc[:, 0:n], [(xn_cols(c, b), w(c)) for c in range(CH)],
                            [xnT_ready[b], t_routers, *free["B_sc"]], "logits")

        def ffn0(done_at, base):
            gate = gates[:, 4:5]
            hsT_state = {}

            def low(b):
                (hg, t_hg) = piece(base)
                t = products(B_sc[:, 0:HL + E0], [(xn_cols(c, b), tuple(m[:, c * (HL + E0):(c + 1) * (HL + E0)] for m in hg))
                                                  for c in range(CH)], [xnT_ready[b], t_hg, *free["B_sc"]], "low_rank")
                if b == NB - 1:
                    hsT_state["hg_done"] = t
                chain(lambda e: e.tensor_copy(rt[:, 0, :], B_sc[:, HL:HL + E0]), t)
                first_max(rt[:, 1, :], r1[:, 0:1], rt[:, 0, :], E0)
                second_max(rt[:, 2, :], r1[:, 1:2], rt[:, 1, :], rt[:, 0, :], E0)
                t = chain(lambda e: e.tensor_tensor(r1[:, 2:3], r1[:, 1:2], r1[:, 0:1], ALU.subtract))
                t = put("act", lambda e: e.activation(r1[:, 3:4], r1[:, 2:3], ACT.Exp), [t], "route_exp")
                chain(lambda e: e.tensor_scalar(r1[:, 4:5], r1[:, 3:4], 1.0, None, ALU.add), t)
                chain(lambda e: e.reciprocal(r1[:, 5:6], r1[:, 4:5]))
                chain(lambda e: e.tensor_tensor(r1[:, 6:7], r1[:, 3:4], r1[:, 5:6], ALU.mult))
                chain(lambda e: e.tensor_scalar(rt[:, 3, :], rt[:, 1, :], r1[:, 5:6], LORA_SCALE, ALU.mult, ALU.mult))
                chain(lambda e: e.tensor_scalar(rt[:, 4, :], rt[:, 2, :], r1[:, 6:7], LORA_SCALE, ALU.mult, ALU.mult))
                chain(lambda e: e.tensor_tensor(rt[:, 3, :], rt[:, 3, :], rt[:, 4, :], ALU.add))
                t = chain(lambda e: e.tensor_tensor(
                    hs[:, :].rearrange("p (e r) -> p e r", r=RANK), B_sc[:, 0:HL].rearrange("p (e r) -> p e r", r=RANK),
                    rt[:, 3, :].unsqueeze(2).to_broadcast([P, E0, RANK]), ALU.mult), *free["hs"])
                free["B_sc"] = [t]
                hsT_state["hs"] = t

            HH = HL // 2

            def turn(b):
                for k in range(2):
                    t = put("pe", lambda e, k=k: e.transpose(B_oT[0:HH, k * P:(k + 1) * P], hs[:, k * HH:(k + 1) * HH],
                                                             ident[:, :]),
                            [hsT_state["hs"], *free["B_oT"]] if k == 0 else (), "hs_turn" if k == 1 else None)
                free["hs"] = [t]
                hsT_state["hsT"] = split(B_oT[0:HH, 0:2 * P], hsT[0][:, :], hsT[1][:, :],
                                         [t, *free["spare"]], "hsT")
                free["B_oT"] = [hsT_state["hsT"]]

            def out(b, now):
                (lb, t_lb), (w0, tw0), (w1, tw1) = piece(base + 1), piece(base + 2), piece(base + 3)
                pairs = [(xn_cols(c, b), tuple(m[:, (c % 2) * D:(c % 2 + 1) * D] for m in (w0, w1)[c // 2])) for c in range(CH)]
                pairs += [(tuple(m[:, k * P:(k + 1) * P] for m in hsT), tuple(m[0:HH, k * D:(k + 1) * D] for m in lb))
                          for k in range(2)]
                t = products(B_out[:, :], pairs, [hsT_state["hsT"], t_lb, tw0, tw1, *free["B_out"]], "ffn0")
                free["spare"] = [t]
                xnT_free[b] = t
                if b == NB - 1:
                    for m in range(4):
                        release(base + m, t, now)
                add_to_x(b, B_out, "B_out", gate, t)

            for b in range(NB):
                i = done_at[b]
                at(i, 8, ln_stats, b)
                at(i, 35, ln_turn, b)
                at(i + 1, 65, low, b)
                at(i + 2, 65 - 1, turn, b)
                at(i + 3, 2, out, b, i + 3)
            return [i + 3 for i in done_at]

        def ffn1(done_at, base):
            gate = gates[:, 5:6]

            def out(b, now):
                (w0, tw0), (w1, tw1) = piece(base), piece(base + 1)
                pairs = [(xn_cols(c, b), tuple(m[:, (c % 2) * D:(c % 2 + 1) * D] for m in (w0, w1)[c // 2])) for c in range(CH)]
                t = products(B_out[:, :], pairs, [xnT_ready[b], tw0, tw1, t_biases, *free["B_out"]], "ffn1",
                             more=[(last_row[:, :], bias[0][:, :]), (last_row[:, :], bias[1][:, :])])
                xnT_free[b] = t
                if b == NB - 1:
                    release(base, t, now)
                    release(base + 1, t, now)
                add_to_x(b, B_out, "B_out", gate, t)

            for b in range(NB):
                i = done_at[b]
                at(i, 8, ln_stats, b)
                at(i, 35, ln_turn, b)
                at(i + 2, 2, out, b, i + 2)
            return [i + 2 for i in done_at]

        def ffn2(done_at, base):
            gate = gates[:, 6:7]
            comb_ready = [None] * NB

            def route(b):
                bank = B_sc[:, 0:E2]
                t = router_logits(b, 0, E2)
                t = softmax_rows(rt[:, 1, 0:E2], bank, E2, t)
                free["B_sc"] = [t]
                first_max(rt[:, 2, 0:E2], r1[:, 3:4], rt[:, 1, 0:E2], E2)
                second_max(rt[:, 3, 0:E2], r1[:, 4:5], rt[:, 2, 0:E2], rt[:, 1, 0:E2], E2)
                chain(lambda e: e.tensor_tensor(r1[:, 5:6], r1[:, 3:4], r1[:, 4:5], ALU.add))
                chain(lambda e: e.reciprocal(r1[:, 6:7], r1[:, 5:6]))
                chain(lambda e: e.tensor_scalar(r1[:, 7:8], r1[:, 3:4], r1[:, 6:7], gate, ALU.mult, ALU.mult), t_tanh)
                chain(lambda e: e.tensor_scalar(r1[:, 8:9], r1[:, 4:5], r1[:, 6:7], gate, ALU.mult, ALU.mult))
                chain(lambda e: e.tensor_scalar(rt[:, 4, 0:E2], rt[:, 3, 0:E2], r1[:, 8:9], None, ALU.mult))
                comb_ready[b] = chain(lambda e: e.scalar_tensor_tensor(out=comb[:, b, :], in0=rt[:, 2, 0:E2],
                                                                       scalar=r1[:, 7:8], in1=rt[:, 4, 0:E2],
                                                                       op0=ALU.mult, op1=ALU.add))

            experts = SHARED_TILES + E2
            steps = [(e, half) for e in range(experts) for half in range(2)]
            HB = NB // 2
            acts = [pT, oT]
            act_ready = {}
            banks = [(B_out, "B_out"), (B_sc, "B_sc"), (B_pt, "B_pt"), (B_oT, "B_oT")]

            def gu_piece(e):
                return base + 3 * (e // 2) + e % 2

            def up(n, now):
                e, half = steps[n]
                w, tw = piece(gu_piece(e))
                bank, name = ((B_qkv, "B_qkv"), (B_qkT, "B_qkT"))[n % 2]
                tokens = slice(half * HB * P, (half + 1) * HB * P)
                ready = xnT_ready[half * HB:(half + 1) * HB]
                tok = []
                for j in range(2):
                    wj = [tuple(m[:, c * 2 * P + j * P:c * 2 * P + (j + 1) * P] for m in w) for c in range(CH)]
                    tok.append(products(bank[:, j * 512:(j + 1) * 512], [(wj[c], tuple(m[:, c, tokens] for m in xnT))
                                                                         for c in range(CH)],
                                        [tw, *ready, *free[name]], "gate_up"))
                if half == 1:
                    release(gu_piece(e), tok[1], now)
                for b in range(half * HB, (half + 1) * HB):
                    xnT_free[b] = tok[1]
                k = n % 2
                th, sg = S[:, k, :], W[:, k, :]
                t = put("act", lambda e: e.activation(th, bank[:, 0:512], ACT.Tanh, scale=0.5), [tok[0], *free[f"S{k}"]], "silu")
                t = put("dve", lambda e: e.scalar_tensor_tensor(out=sg, in0=th, scalar=1.0, in1=bank[:, 0:512], op0=ALU.add,
                                                                op1=ALU.mult), [t, *free[f"W{k}"]], "silu")
                t = put("dve", lambda e: e.scalar_tensor_tensor(out=th, in0=sg, scalar=0.5, in1=bank[:, 512:1024],
                                                                op0=ALU.mult, op1=ALU.mult), [t, tok[1]], "act")
                free[name] = [t]
                free[f"W{k}"] = [t]
                dst = acts[k]
                h = put("act", act_copy(dst[0][:, :], th), [t, *free[("pT", "oT")[k]]], "act_hi")
                t = put("dve", sub(dst[1][:, :], th, f32(dst[0][:, :])), [h], "act_lo")
                free[f"S{k}"] = [t]
                act_ready[n] = t

            def down(n, now):
                e, half = steps[n]
                nd = base + 3 * (e // 2) + 2
                w, tw = piece(nd)
                wd = tuple(m[:, (e % 2) * D:(e % 2 + 1) * D] for m in w)
                k = n % 2
                for j in range(HB):
                    b = half * HB + j
                    bank, name = banks[j]
                    t = products(bank[:, :], [(tuple(m[:, j * P:(j + 1) * P] for m in acts[k]), wd)],
                                 [act_ready[n], tw, *free[name]], "down")
                    if e < SHARED_TILES:
                        add_to_x(b, bank, name, gate, t)
                    else:
                        add_to_x(b, bank, name, comb[:, b, e - SHARED_TILES:e - SHARED_TILES + 1], t, [comb_ready[b]])
                free[("pT", "oT")[k]] = [t]
                if half == 1 and e % 2 == 1:
                    release(nd, t, now)

            for b in range(NB):
                at(done_at[b], 8, ln_stats, b)
                at(done_at[b], 35, ln_turn, b)
                at(done_at[b] + 1, 65, route, b)
            first = done_at[-1] + 2
            for n in range(len(steps)):
                at(first + n, 70, up, n, first + n)
                at(first + n + 1, 75, down, n, first + n + 1)
            last = first + len(steps) - 1
            return [last + 1 + b for b in range(NB)]

        def ffn3(done_at, base):
            gate = gates[:, 7:8]
            comb_ready = [None] * NB
            banks = [(B_out, "B_out"), (B_oT, "B_oT")]

            def route(b):
                t = router_logits(b, E2, E3)
                free["B_sc"] = [chain(lambda e: e.tensor_tensor(rt[:, 4, 0:E3], B_sc[:, 0:E3], gate_b[:, :], ALU.add),
                                      t, t_gate_b)]
                softmax_rows(rt[:, 1, 0:E3], rt[:, 4, 0:E3], E3, None)
                first_max(rt[:, 2, 0:E3], r1[:, 3:4], rt[:, 1, 0:E3], E3)
                t = rt_done[0]
                comb_ready[b] = chain(lambda e: e.tensor_scalar(comb[:, b, 0:E3], rt[:, 2, 0:E3], gate, None, ALU.mult),
                                      t_tanh)
                t = put("pe", lambda e: e.transpose(B_pt[0:E3, 0:P], rt[:, 2, 0:E3], ident[:, :]), [t, *free["B_pt"]],
                        "onehot_turn")
                rt_done[0] = put("dve", lambda e: e.tensor_copy(onehotT, B_pt[0:E3, 0:P]),
                                 [t, comb_ready[b], *free["onehotT"]], "route")
                free["B_pt"] = [rt_done[0]]
                t = products(B_oT[:, :], [], [rt_done[0], t_biases, *free["B_oT"]], "bias3",
                             more=[(onehotT, bias[0][0:E3, :]), (onehotT, bias[1][0:E3, :])])
                free["onehotT"] = [t]
                add_to_x(b, B_oT, "B_oT", gate, t)

            def expert(e3, b, now):
                n = base + 2 * e3
                (w0, tw0), (w1, tw1) = piece(n), piece(n + 1)
                pairs = [(xn_cols(c, b), tuple(m[:, (c % 2) * D:(c % 2 + 1) * D] for m in (w0, w1)[c // 2])) for c in range(CH)]
                bank, name = banks[b % 2]
                t = products(bank[:, :], pairs, [tw0, tw1, *free[name]], "ffn3")
                if b == NB - 1:
                    release(n, t, now)
                    release(n + 1, t, now)
                add_to_x(b, bank, name, comb[:, b, e3:e3 + 1], t, [comb_ready[b]])

            for b in range(NB):
                at(done_at[b], 8, ln_stats, b)
                at(done_at[b], 35, ln_turn, b)
                at(done_at[b] + 1, 65, route, b)
            first = done_at[0] + 3
            for e3 in range(E3):
                for b in range(NB):
                    i = max(first + e3 * NB + b, done_at[b] + 3)
                    at(i, 70, expert, e3, b, i)
            return [first + (E3 - 1) * NB + b for b in range(NB)]

        now, at_piece = 1, 0
        done_at = [0] * NB
        for s in range(sublayers):
            layer = s // 2
            if s % 2 == 0:
                n_pieces = 5 if layer == 2 else 5 * G
                for b in range(NB):
                    at(done_at[b] if s else b, 36, ln_stats, b)
                    at((done_at[b] if s else b) + 1, 7, ln_turn, b)
                first = (1 if s == 0 else max(done_at[b] + 1 - (b if layer != 2 else G * b) for b in range(NB)))
                first += (1, 5, 3, 0)[layer]
                plan += [("float", at_piece + m) for m in range(n_pieces)]
                done_at = attention(layer, first, len(plan) - n_pieces)
                at_piece += n_pieces
            else:
                n_pieces = (4, 2, 3 * (SHARED_TILES + E2) // 2, 2 * E3)[layer]
                if layer == 1:
                    plan += [("quantised", m) for m in range(2)]
                else:
                    plan += [("float", at_piece + m) for m in range(n_pieces)]
                    at_piece += n_pieces
                done_at = (ffn0, ffn1, ffn2, ffn3)[layer](done_at, len(plan) - n_pieces)

        advance(0, 3)
        for i in range(max(events) + 1):
            for _, _, what, args in sorted(events[i], key=lambda x: x[:2]):
                what(*args)
            advance(i, 2 if i < 4 else 1)
        assert len(held) == len(plan)

        for b in range(NB):
            put("sync", lambda e, b=b: e.dma_start(out[b], X[:, b, :]), [x_done[b]], "store", 16)
        qs.wait_all("sync", ("sync_store", "sync_raw", "sync_groupcols", "act_small", "pool_rope"))

        block = ctx.enter_context(nc.Block())
        block.sync(lambda e: qs.emit("sync", e))
        block.scalar(lambda e: qs.emit("act", e))
        block.vector(lambda e: qs.emit("dve", e))
        block.gpsimd(lambda e: qs.emit("pool", e))
        block.tensor(lambda e: qs.emit("pe", e))


def _chunks(w):
    return w.reshape(CH, P, -1).transpose(1, 0, 2)


def _two(w):
    return [w[:, 0:2].reshape(P, PIECE), w[:, 2:4].reshape(P, PIECE)]


def _pad(w):
    full = np.zeros((P, PIECE), np.float32)
    full[:w.shape[0], :w.shape[1]] = w
    return full


def _attention_pieces(wq, wk, wv, wo):
    out = []
    for g in range(wq.shape[1]):
        out += _two(_chunks(wq[:, g]))
        out.append(np.concatenate([_chunks(wk[:, g]), _chunks(wv[:, g])], axis=2).reshape(P, PIECE))
        out += _two(wo[g].transpose(1, 0, 2))
    return out


def _big(wq, wk, wv, wo):
    return _attention_pieces(wq.reshape(D, G, HG), wk.reshape(D, G, P), wv.reshape(D, G, P), wo.reshape(G, R, P, D))


def _layout(i):
    pieces = _big(i["L0_xattn_Wq"], i["L0_xattn_Wk"], i["L0_xattn_Wv"], i["L0_xattn_Wo"])
    low = np.concatenate([i["L0_ffn_lora_A"].reshape(HL, D).T, i["L0_ffn_gate_W"].T], axis=1)
    pieces.append(_pad(_chunks(low).reshape(P, -1)))
    lora_b = i["L0_ffn_lora_B"].transpose(0, 2, 1).reshape(2, HL // 2, D).transpose(1, 0, 2).reshape(HL // 2, 2 * D)
    pieces.append(_pad(lora_b))
    pieces += _two(_chunks(i["L0_ffn_base_W"].T))
    pieces += _big(*(i[f"L1_xattn_{k}_proj_w"].T for k in "qkvo"))
    hd = D // (G * R)
    wq = i["L2_xattn_w_q"].T.reshape(D, G, R, hd).transpose(0, 2, 1, 3).reshape(D, 1, D)
    wo = i["L2_xattn_w_out"].T.reshape(G, R, hd, D).transpose(1, 0, 2, 3).reshape(1, R, P, D)
    pieces += _attention_pieces(wq, i["L2_xattn_w_k"].T.reshape(D, 1, P), i["L2_xattn_w_v"].T.reshape(D, 1, P), wo)
    sgu, sdn = i["L2_ffn_shared_w_gate_up"], i["L2_ffn_shared_w_down"]
    gu = [np.concatenate([sgu[k * P:(k + 1) * P], sgu[D + k * P:D + (k + 1) * P]]).T for k in range(SHARED_TILES)]
    gu += [w.T for w in i["L2_ffn_w_gate_up"]]
    dn = [sdn[:, k * P:(k + 1) * P].T for k in range(SHARED_TILES)] + [w.T for w in i["L2_ffn_w_down"]]
    for e in range(0, SHARED_TILES + E2, 2):
        pieces += [_chunks(gu[e]).reshape(P, PIECE), _chunks(gu[e + 1]).reshape(P, PIECE),
                   np.concatenate([dn[e], dn[e + 1]], axis=1)]
    pieces += _big(*(i[f"L3_xattn_W{k}"].T for k in "qkvo"))
    for w in i["L3_ffn_expert_w"]:
        pieces += _two(_chunks(w.T))

    freq = (1.0 / THETA ** (np.arange(0, P, 2, dtype=np.float32) / np.float32(P))).astype(np.float32)
    angle = np.arange(MAX_POS, dtype=np.float32)[:, None] * freq[None, :]
    cos, sin = np.cos(angle), np.sin(angle)
    groups = np.arange(P) // hd

    def grouped(z):
        return np.stack(_two(_chunks(np.repeat(z.reshape(D, D // 32).T, 32, axis=0))))

    return {
        "pieces": np.stack(pieces),
        "ctxT": i["ctx_4096"].reshape(T, D).T.reshape(CH, P, T),
        "routers": np.concatenate([_chunks(i["L2_ffn_gate_w"].T).reshape(P, -1),
                                   _chunks(i["L3_ffn_gate_w"].T).reshape(P, -1)], axis=1),
        "quant": np.stack(_two(_chunks(i["L1_ffn_qweight"].T))),
        "zeros": grouped(i["L1_ffn_zeros"]),
        "scales": grouped(i["L1_ffn_scales"]),
        "x": i["x"],
        "g_xattn": i["g_xattn"],
        "g_ffn": i["g_ffn"],
        "pos": i["pos_BxS2"].T,
        "mask0": i["mask_BxSxS2_ik0"].transpose(1, 0, 2).reshape(P, NB * P),
        "mask13": i["mask_1x1xSxS2_ff0"].reshape(P, P),
        "mask2": i["mask_SxS2_bk0"].view(np.int32),
        "norm_w": np.stack([i["L1_xattn_q_norm_w"], i["L3_xattn_q_norm_w"], i["L1_xattn_k_norm_w"],
                            i["L3_xattn_k_norm_w"]])[:, :, None],
        "bias": np.concatenate([i["L3_ffn_expert_b"], i["L1_ffn_bias"][None, :]]),
        "last_row": np.repeat(np.eye(E3 + 1, dtype=np.float32)[:, E3:], P, axis=1),
        "gate_b": i["L3_ffn_gate_b"],
        "rope": np.concatenate([cos, cos, -sin, sin], axis=1).astype(np.float32),
        "ident": np.eye(P, dtype=np.float32),
        "groupmask": (groups[:, None] == np.arange(G)[None, :]).astype(np.float32),
        "groupcols": (groups[None, :] == np.arange(G)[:, None]).astype(np.float32).reshape(G * P),
        "rev": (E0 - np.arange(E0)).astype(np.float32),
    }


def kernel(sublayers=8, **inputs):
    import concourse.bacc as _bacc
    from concourse.bass_utils import run_bass_kernel_spmd as _run

    nc = _bacc.Bacc("TRN2", target_bir_lowering=False, num_devices=1)
    arrays = {f"in_{n}": np.ascontiguousarray(a) for n, a in _layout({k: np.asarray(v) for k, v in inputs.items()}).items()}
    io = {n[3:]: nc.dram_tensor(n, a.shape, mybir.dt.from_np(a.dtype), kind="ExternalInput").ap() for n, a in arrays.items()}
    io["groupcols"] = io["groupcols"].rearrange("(a n) -> a n", a=4)
    out = nc.dram_tensor("out_x", (NB, P, D), F32, kind="ExternalOutput").ap()
    build(nc, io, out, sublayers)
    r = _run(nc, [arrays], core_ids=[0])
    return r.results[0]["out_x"]
```

```python
from collections import defaultdict
from contextlib import ExitStack

import numpy as np
import concourse.bass as bass
from concourse import mybir

F32 = mybir.dt.float32
F32R = mybir.dt.float32r
I32 = mybir.dt.int32
U8 = mybir.dt.uint8
I8 = mybir.dt.int8
ALU = mybir.AluOpType
ACT = mybir.ActivationFunctionType
AX = mybir.AxisListType.X

P = 128
NB = 8
T = NB * P
D = 512
CH = D // P
G = 8
R = 4
HG = R * P
PIECE = 1024
HALF = PIECE // 2
SLOTS = 9
RAWS = 2
EPS = 1e-5
MASKED = -1e9
FMIN = float(np.finfo(np.float32).min)
MAX_POS, THETA = 512, 10000.0
E0, RANK, LORA_SCALE = 28, 8, 2.0
E2, SHARED_TILES = 16, 4
E3 = 8
LO_ROW = 32
HL = E0 * RANK
VSLOTS = 6
LANDING = 0.4
FAR = -3.0e38


class Queues:

    def __init__(self, new_semaphore):
        self.new_semaphore = new_semaphore
        self.sems, self.count = {}, defaultdict(int)
        self.items = {e: [] for e in ("sync", "act", "dve", "pool", "pe")}
        self.passed = {e: {} for e in self.items}

    def put(self, engine, issue, after=(), done=None, by=1):
        for token in after:
            if token is None:
                continue
            name, value = token
            if self.passed[engine].get(name, 0) < value:
                self.passed[engine][name] = value
                self.items[engine].append((None, name, value))
        if done is not None:
            done = f"{engine}_{done}"
            if done not in self.sems:
                self.sems[done] = self.new_semaphore(done)
            self.count[done] += by
        self.items[engine].append((issue, done, by))
        return (done, self.count[done]) if done else None

    def wait_all(self, engine, prefixes):
        for name, value in self.count.items():
            if name.startswith(prefixes):
                self.items[engine].append((None, name, value))

    def emit(self, engine, eng):
        for issue, name, n in self.items[engine]:
            if issue is None:
                eng.wait_ge(self.sems[name], n)
            else:
                ins = issue(eng)
                if name is not None:
                    ins.then_inc(self.sems[name], n)


def build(nc, io, out, sublayers=8):
    with ExitStack() as ctx:
        def sb(name, shape, dt=F32):
            return ctx.enter_context(nc.sbuf_tensor(name, shape, dt))

        def pb(name, width):
            return ctx.enter_context(nc.psum_tensor(name, [P, width], F32))

        def new_semaphore(name):
            return ctx.enter_context(nc.semaphore(name))

        qs = Queues(new_semaphore)
        put = qs.put

        X = sb("X", [P, NB, D])
        xnT = [sb(f"xnT_{k}", [P, CH, T], F32R) for k in "hl"]
        ctxT = [sb(f"ctxT_{k}", [P, CH, T], F32R) for k in "hl"]
        ring = [sb(f"ring_{k}", [P, SLOTS, PIECE], F32R) for k in "hl"]
        qk = sb("qk", [P, (R + 1) * P])
        sq = sb("sq", [P, (R + 1) * P])
        qT = [sb(f"qT_{k}", [P, HG], F32R) for k in "hl"]
        kT = [sb(f"kT_{k}", [P, P], F32R) for k in "hl"]
        v = [sb(f"v_{k}", [P, VSLOTS, P], F32R) for k in "hl"]
        spare = [sb(f"spare_{k}", [P, 2 * P], F32R) for k in "hl"]
        hsT = [m[0:HL // 2, :] for m in spare]
        vall = [m[:, 0:P] for m in spare]
        S = sb("S", [P, 2, HG])
        W = sb("W", [P, 2, HG])
        pT = [sb(f"pT_{k}", [P, HG], F32R) for k in "hl"]
        oT = [sb(f"oT_{k}", [P, HG], F32R) for k in "hl"]
        tables = sb("tables", [P, NB, P])
        mask0 = [sb("mask0_keep", [P, NB, P], I8), sb("mask0_minus", [P, NB, P], I8)]
        mask2 = mask0[0][:, :, :].rearrange("p b k -> p (b k)").bitcast(F32)[:, 0:P]
        mask13 = sb("mask13", [P, P])
        mask2u = sb("mask2u", [P, P], U8)
        ident = sb("ident", [P, P])
        xn = sb("xn", [P, 2, D])
        raw = sb("raw", [P, RAWS, HALF])
        routers = [sb(f"routers_{k}", [P, CH * (E2 + E3)], F32R) for k in "hl"]
        bias = sb("bias", [LO_ROW + E3 + 1, D], F32R)
        pick1 = spare[1][0:LO_ROW + E3 + 1, P:2 * P]
        choiceT = spare[0][0:LO_ROW + E3 + 1, P:2 * P]
        gates = sb("gates", [P, 8])
        comb = sb("comb", [P, NB, E2])
        pos = sb("pos", [P, NB], I32)
        norm_w = sb("norm_w", [P, 4])
        wqk = sb("wqk", [P, 2])
        groupmask = sb("groupmask", [P, G])
        gate_b = sb("gate_b", [P, E3])
        rev = sb("rev", [P, E0])
        pw = sb("pw", [P, 8])
        st6 = sb("st6", [P, 6])
        mv = sb("mv", [P, 2, 2])
        rstd = sb("rstd", [P, 2, 2])
        ss = sb("ss", [P, 8])
        rn = sb("rn", [P, 2, 8])
        nmx = sb("nmx", [P, 2, R])
        den = sb("den", [P, 2, R])
        rden = sb("rden", [P, 2, R])
        rt = sb("rt", [P, 8, E0])
        r1 = sb("r1", [P, 16])
        hs = sb("hs", [P, 2, HL])
        choice = hs[:, 0, 0:LO_ROW + E3 + 1]

        B_qkv = pb("B_qkv", 1024)
        B_qkT = pb("B_qkT", 1024)
        B_sc = pb("B_sc", 512)
        B_pt = pb("B_pt", 512)
        B_oT = pb("B_oT", 512)
        B_out = pb("B_out", 512)
        free = defaultdict(list)

        def f32(ap):
            return ap.bitcast(F32)

        def act_copy(dst, src, scale=1.0):
            return lambda e: e.activation(dst, src, ACT.Copy, scale=scale)

        def sub(dst, a, b):
            return lambda e: e.tensor_tensor(dst, a, b, ALU.subtract)

        def split(bank, hi, lo, after, name, scale=1.0):
            h = put("act", act_copy(hi, bank, scale), after, f"{name}_hi")
            if isinstance(scale, float):
                return put("dve", sub(lo, bank, f32(hi)), [h], f"{name}_lo")
            return put("dve", lambda e: e.scalar_tensor_tensor(out=lo, in0=bank, scalar=scale, in1=f32(hi),
                                                               op0=ALU.mult, op1=ALU.subtract), [h], f"{name}_lo")

        def products(dst, pairs, after, done=None, more=()):
            steps = []
            for (ah, al), (bh, bl) in pairs:
                steps += [(ah, bh), (ah, bl), (al, bh)]
            steps += more
            token = None
            for n, (a, b) in enumerate(steps):
                token = put("pe", lambda e, a=a, b=b, n=n: e.matmul(dst, a, b, start=n == 0, stop=n == len(steps) - 1),
                            after if n == 0 else (), done if n == len(steps) - 1 else None)
            return token

        plan = []
        landing = []
        ready = {}
        slot_of = {}
        slot_free = [(s, None, -1) for s in range(SLOTS)]
        asked = [0]
        raw_free = [None] * RAWS
        raw_next, raw_left = [0], [RAWS]

        scales = [tables[:, :, :].rearrange("p a n -> p (a n)")[:, h * HALF:(h + 1) * HALF] for h in range(2)]

        def need(rows, iteration, order, kind="float"):
            numbers = [asked[0] + m for m in range(len(rows))]
            asked[0] += len(rows)
            plan.extend((iteration, order, n, half, kind, row) for n, row in zip(numbers, rows)
                        for half in range(2 if kind in ("float", "quantised") else 1))
            return numbers

        def fetch(now):
            while plan:
                _, _, n, half, kind, row = item = plan[0]
                cols = slice(half * HALF, (half + 1) * HALF)
                if kind == "quantised":
                    sources = [io["quant"][row][:, cols], io["zeros"][row][:, cols]]
                elif kind == "routers":
                    sources = [io["routers"]]
                else:
                    sources = [io["pieces"][row][:, cols] if kind == "float" else io["ctxT"][row]]
                if raw_left[0] < len(sources):
                    return
                raws, tokens = [], []
                for m, src in enumerate(sources):
                    k = raw_next[0] % RAWS
                    raw_next[0] += 1
                    raw_left[0] -= 1
                    dst = raw[:, k, 0:src.shape[1]]
                    dst = dst.bitcast(I32) if kind == "quantised" and m == 0 else dst
                    tokens.append(put("sync", lambda e, dst=dst, src=src: e.dma_start(dst, src), [raw_free[k]], f"raw{k}", 16))
                    raws.append(k)
                if kind == "quantised":
                    tokens.append(put("sync", lambda e, half=half, src=io["scales"][row][:, cols]: e.dma_start(scales[half], src),
                                      free["tables"], "scales", 16))
                landing.append((now, item, raws, tokens))
                plan.pop(0)

        def split_next(now, engine):
            if not landing:
                return
            when, (_, _, n, half, kind, row), raws, tokens = landing[0]
            if now is not None and when is not None and now - when < LANDING:
                return
            released = None
            if kind in ("float", "quantised"):
                if half == 0:
                    if not slot_free or (now is not None and slot_free[0][2] >= now - LANDING):
                        return
                    slot_of[n], released, _ = slot_free.pop(0)
                hi, lo = (m[:, slot_of[n], half * HALF:(half + 1) * HALF] for m in ring)
            elif kind == "ctx":
                hi, lo = (m[:, :, row * P:(row + 1) * P] for m in ctxT)
            else:
                hi, lo = (m[:, :] for m in routers)
            landing.pop(0)
            src = raw[:, raws[0], 0:hi.shape[1] if kind == "routers" else HALF]
            if kind == "quantised":
                zeros = raw[:, raws[1], :]
                t = put("dve", lambda e: e.tensor_tensor(src, src.bitcast(I32), zeros, ALU.subtract), tokens[0:2], "dequant")
                t = put("dve", lambda e: e.tensor_tensor(src, src, scales[half], ALU.mult), [t, tokens[2]], "dequant")
                raw_free[raws[1]] = t
                free["tables"] = [t]
                tokens = [t]
            if kind == "ctx":
                src = src.rearrange("p (c t) -> p c t", c=CH)
            h = put("act", act_copy(hi, src), [*tokens, released], "piece_hi")
            t = put(engine, sub(lo, src, f32(hi)), [h], "piece_lo")
            raw_free[raws[0]] = t
            raw_left[0] += len(raws)
            ready.setdefault(n, []).append(t)

        def arrive(n, items):
            while len(ready.get(n, ())) < items:
                before = len(plan) + len(landing)
                fetch(None)
                split_next(None, "pool")
                assert len(plan) + len(landing) < before, f"no slot for piece {n}"
            return ready[n]

        def piece(n):
            tokens = arrive(n, 2)
            return tuple(m[:, slot_of[n], :] for m in ring), tokens

        def release(n, token, now):
            slot_free.append((slot_of[n], token, now))

        small = [0]

        def small_load(dst, src, after=()):
            small[0] += 1
            return put("act", lambda e: e.dma_start(dst, src), after, f"small{small[0]}", 16)

        def rows(vec, n=P):
            return vec.partition_broadcast(n)

        x_done = [None] * NB

        def load_x(b):
            x_done[b] = small_load(X[:, b, :], io["x"][b])

        load_x(0)
        t_ident = small_load(ident[:, :], io["ident"])
        t_gates = [small_load(gates[:, 0:4], rows(io["g_xattn"])), small_load(gates[:, 4:8], rows(io["g_ffn"]))]
        t_pos = small_load(pos[:, :], io["pos"])
        t_m0 = small_load(S[:, :, :].rearrange("p s n -> p (s n)").bitcast(I32), io["mask0"])
        t_m13 = small_load(mask13[:, :], io["mask13"])
        t_m2 = small_load(mask2u[:, :].bitcast(I32), io["mask2"])
        t_nw = [small_load(norm_w[:, n:n + 1], io["norm_w"][n]) for n in range(4)]
        t_gm = small_load(groupmask[:, :], io["groupmask"])
        t_gate_b = small_load(gate_b[:, :], rows(io["gate_b"]))
        t_rev = small_load(rev[:, :], rows(io["rev"]))
        biases = W[0:LO_ROW + E3 + 1, 0, :]
        t_bias = small_load(biases, io["bias"])
        t_tanh = put("act", lambda e: e.activation(gates[:, :], gates[:, :], ACT.Tanh), t_gates, "tanh_gates")
        t_pw = put("pool", lambda e: e.memset(pw[:, :], -0.5), (), "const")
        t = put("dve", lambda e: e.tensor_scalar(mask0[0][:, :, :], S[:, :, :].rearrange("p s (b k) -> p (s b) k", k=P)
                                                 .bitcast(I32), 0.0, None, ALU.not_equal), [t_m0], "const")
        free["S0"] = free["S1"] = [t]
        t_mask0 = put("dve", lambda e: e.tensor_scalar(mask0[1][:, :, :], mask0[0][:, :, :], -1.0, None, ALU.add),
                      [t], "const")
        t_wqk = put("dve", lambda e: e.tensor_tensor(wqk[:, :], norm_w[:, 0:2], norm_w[:, 2:4], ALU.mult), t_nw, "const")
        t = put("dve", lambda e: e.tensor_copy(bias[:, :], biases), [t_bias], "const")
        t_biases = put("dve", sub(bias[LO_ROW:, :], biases[LO_ROW:, :], f32(bias[LO_ROW:, :])), [t], "const")
        free["W0"] = free["W1"] = [t_biases]
        t_rope = []
        for b in range(NB):
            t_rope.append(put("pool", lambda e, b=b: e.indirect_dma_start(
                out=tables[:, b, :], out_offset=None, in_=io["rope"],
                in_offset=bass.IndirectOffsetOnAxis(ap=pos[:, b:b + 1], axis=0)), [t_pos], f"rope{b}", 16))
        xnT_free = [None] * NB
        xnT_ready = [None] * NB
        xn_ready = [None] * NB
        norms = [0]

        def ln_stats(b):
            k = norms[0] % 2
            norms[0] += 1
            t = put("dve", lambda e: e.bn_stats(st6[:, :], X[:, b, :]), [x_done[b], *free["st6"]], "ln")
            t = put("dve", lambda e: e.bn_aggr(mv[:, k, :], st6[:, :]), [t, *free[f"mv{k}"]], "ln")
            free["st6"] = [t]
            t2 = put("pool", lambda e: e.tensor_scalar(rstd[:, k, 0:1], mv[:, k, 1:2], EPS, 1.0, ALU.add, ALU.mult), [t], "ln")
            xn_ready[b] = k, put("pool", lambda e: e.tensor_tensor(rstd[:, k, 1:2], rstd[:, k, 0:1], pw[:, 0:1], ALU.pow),
                                 [t2, t_pw], "ln")

        def ln_apply(b):
            k, t2 = xn_ready[b]
            t = put("dve", lambda e: e.tensor_scalar(xn[:, k, :], X[:, b, :], mv[:, k, 0:1], rstd[:, k, 1:2],
                                                     ALU.subtract, ALU.mult), [t2, *free[f"xn{k}"]], "ln")
            free[f"mv{k}"] = [t]
            xn_ready[b] = k, t

        def ln_turn(b):
            k, ready = xn_ready[b]
            for c in range(CH):
                t = put("pe", lambda e, c=c: e.transpose(B_pt[:, c * P:(c + 1) * P], xn[:, k, c * P:(c + 1) * P], ident[:, :]),
                        [ready, t_ident, *free["B_pt"]] if c == 0 else (), "ln_turn" if c == CH - 1 else None)
            free[f"xn{k}"] = [t]
            cols = slice(b * P, (b + 1) * P)
            bank = B_pt[:, :].rearrange("p (c t) -> p c t", c=CH)
            t = split(bank, xnT[0][:, :, cols], xnT[1][:, :, cols], [t, *([xnT_free[b]] if xnT_free[b] else [])], "xnT")
            free["B_pt"] = [t]
            xnT_ready[b] = t

        def xn_cols(c, b):
            return tuple(m[:, c, b * P:(b + 1) * P] for m in xnT)

        def ctx_cols(c, b):
            return tuple(m[:, c, b * P:(b + 1) * P] for m in ctxT)

        events = defaultdict(list)
        steady = set()

        def at(iteration, order, what, *args):
            events[iteration].append((order, len(events[iteration]), what, args))

        def spread(iteration, order, what, *args):
            parts = what(*args)
            at(iteration, order, next, parts, None)
            for later in (6, 12, 22, 28, 34, 44, 48, 54, 61):
                at(iteration + 1, later, next, parts, None)
            finished.append(parts)

        finished = []

        RUNS = [(g, range(NB)) for g in range(G)]
        UNITS = [(g, b) for g, run in RUNS for b in run]

        def attention(layer, first, base):
            kind = ("rope", "norm", "plain", "norm")[layer]
            scale = 0.25 if kind == "plain" else float(P) ** -0.5
            gate = gates[:, layer:layer + 1]
            small_heads = kind == "plain"
            lag_f = 7 if small_heads else 6
            units = [(g, b) for b in range(NB) for g in range(G)] if small_heads else UNITS
            if small_heads:
                five = need(range(base, base + 3), first, 70) + need(range(base + 3, base + 5), first + G - 1 + lag_f, 0)
                weights = [(five, u == len(units) - G, u == len(units) - 1) for u in range(len(units))]
            else:
                weights = []
                for g, run in RUNS:
                    i, row = first + len(weights), base + 5 * g
                    five = need(range(row, row + 3), i, 70) + need(range(row + 3, row + 5), i + lag_f, 0)
                    weights += [(five, b == run[-1], b == run[-1]) for b in run]
            state = [dict() for _ in units]
            k_scale = wqk[:, layer // 2:layer // 2 + 1] if kind == "norm" else 1.0
            tokens = {}

            def fill_tables():
                tokens["mask2"] = put("dve", lambda e: e.tensor_scalar(mask2, mask2u[:, :], -1.0, -FMIN, ALU.add, ALU.mult),
                                      [t_m2, *free["mask0"]], "mask2")
                tokens["cols"] = put("sync", lambda e: e.dma_start(tables[:, :, :], rows(io["groupcols"])),
                                     free["tables"], "groupcols", 16)

            if small_heads:
                at(first - 1, 90, fill_tables)

            def stage_a(u, now):
                g, b = units[u]
                s = state[u]
                vs = (first + u) % VSLOTS
                if not small_heads or g == 0:
                    five, last, _ = weights[u]
                    (q0, tq0), (q1, tq1), (kv, tkv) = (piece(n) for n in five[0:3])
                    wq = [tuple(m[:, (c % 2) * HG:(c % 2 + 1) * HG] for m in (q0, q1)[c // 2]) for c in range(CH)]
                    wkv = [tuple(m[:, c * 2 * P:(c + 1) * 2 * P] for m in kv) for c in range(CH)]
                    products(B_qkv[:, 0:HG], [(xn_cols(c, b), wq[c]) for c in range(CH)],
                             [xnT_ready[b], *tq0, *tq1, *free["B_qkv"]])
                    t = products(B_qkv[:, HG:HG + 2 * P], [(ctx_cols(c, b), wkv[c]) for c in range(CH)], [*arrive(ctx_items[b], 1), *tkv], "qkv")
                    xnT_free[b] = t
                    if last:
                        for n in five[0:3]:
                            release(n, t, now + 0.7)
                    vbank = B_qkv[:, HG + P:HG + 2 * P]
                    bank = B_qkv[:, 0:HG + P].rearrange("p (h d) -> p h d", d=P)
                    qk3 = qk[:, :].rearrange("p (h d) -> p h d", d=P)
                    sq3 = sq[:, :].rearrange("p (h d) -> p h d", d=P)
                    vdst = [m[:, :] for m in vall] if small_heads else [m[:, vs, :] for m in v]
                    if kind == "norm":
                        t_sq = put("act", lambda e: e.activation(sq[:, :], B_qkv[:, 0:HG + P], ACT.Square),
                                   [t, *free["sq"]], "squares")
                    if kind == "plain":
                        s["qk"] = put("act", act_copy(qk[:, :], B_qkv[:, 0:HG + P]), [t, *free["qk"]], "qk_copy")
                    t_v = split(vbank, vdst[0], vdst[1], [t, *(free["spare"] if small_heads else free[f"v{vs}"])], "v")
                    if kind == "norm":
                        t = put("dve", lambda e: e.tensor_reduce(ss[:, 0:R + 1], sq3, AX, ALU.add),
                                [t_sq, *free["ss"]], "sumsq")
                        free["sq"] = [t]
                        r = (first + u) % 2
                        t = put("pool", lambda e: e.tensor_scalar(rn[:, r, 0:R + 1], ss[:, 0:R + 1], 1.0 / P, EPS,
                                                                  ALU.mult, ALU.add), [t, *free[f"rn{r}"]], "rms")
                        free["ss"] = [t]
                        s["rn"] = put("pool", lambda e: e.tensor_tensor(rn[:, r, 0:R + 1], rn[:, r, 0:R + 1],
                                                                        pw[:, 0:R + 1], ALU.pow), [t, t_pw], "rms")
                    elif kind == "rope":
                        half = P // 2
                        cos = tables[:, b, 0:half].unsqueeze(1).unsqueeze(1).to_broadcast([P, R + 1, 2, half])
                        sin = tables[:, b, half:P].unsqueeze(1).to_broadcast([P, R + 1, half])
                        t1 = put("dve", lambda e: e.tensor_tensor(sq3.rearrange("p h (a d) -> p h a d", a=2),
                                                                  bank.rearrange("p h (a d) -> p h a d", a=2), cos, ALU.mult),
                                 [t_v, t_rope[b], *free["sq"]], "rope")
                        put("dve", lambda e: e.tensor_tensor(qk3[:, :, 0:half], bank[:, :, half:P], sin, ALU.mult),
                            free["qk"])
                        t = put("dve", lambda e: e.tensor_tensor(qk3[:, :, half:P], bank[:, :, 0:half], sin, ALU.mult),
                                (), "rope")
                        free["B_qkv"] = [t]
                        free["tables"] = [t]
                        put("pool", lambda e: e.tensor_tensor(qk3[:, :, 0:half], sq3[:, :, 0:half], qk3[:, :, 0:half],
                                                              ALU.subtract), [t])
                        s["qk"] = put("pool", lambda e: e.tensor_tensor(qk3[:, :, half:P], sq3[:, :, half:P],
                                                                        qk3[:, :, half:P], ALU.add), (), "rope")
                        free["sq"] = [s["qk"]]
                    else:
                        free["B_qkv"] = [t_v]
                    s["v"] = t_v
                    if small_heads:
                        for uu in range(u, u + G):
                            state[uu]["vall"] = t_v
                if small_heads:
                    cols = tables[:, g, :]
                    for m in range(2):
                        t = put("pool", lambda e, m=m: e.tensor_tensor(v[m][:, vs, :], f32(vall[m][:, :]), cols, ALU.mult),
                                [s["vall"], tokens["cols"], *free[f"v{vs}"]], "v_group")
                    s["v"] = t
                    if g == G - 1:
                        free["spare"] = [t]

            def stage_a2(u):
                s = state[u]
                bank = B_qkv[:, 0:HG + P].rearrange("p (h d) -> p h d", d=P)
                r = (first + u) % 2
                s["qk"] = put("dve", lambda e: e.tensor_tensor(
                    qk[:, :].rearrange("p (h d) -> p h d", d=P), bank,
                    rn[:, r, 0:R + 1].unsqueeze(2).to_broadcast([P, R + 1, P]), ALU.mult),
                    [s["rn"], s["v"], *free["qk"]], "qk_norm")
                free["B_qkv"] = free[f"rn{r}"] = [s["qk"]]

            def stage_b(u):
                g, b = units[u]
                s = state[u]
                if not small_heads or g == 0:
                    for h in range(R + 1):
                        t = put("pe", lambda e, h=h: e.transpose(B_qkT[:, h * P:(h + 1) * P], qk[:, h * P:(h + 1) * P],
                                                                 ident[:, :]),
                                [s["qk"], *free["B_qkT"]] if h == 0 else (), "qk_turn" if h == R else None)
                    free["qk"] = [t]
                    s["qT"] = split(B_qkT[:, 0:HG], qT[0][:, :], qT[1][:, :], [t, *free["qT"]], "qT")
                    for uu in range(u, u + G if small_heads else u + 1):
                        state[uu]["turned"], state[uu]["qT"] = t, s["qT"]

            def stage_b_k(u):
                g, b = units[u]
                s = state[u]
                ks = groupmask[:, g:g + 1] if small_heads else k_scale
                s["kT"] = split(B_qkT[:, HG:HG + P], kT[0][:, :], kT[1][:, :],
                                [s["turned"], t_gm, t_wqk, *free["qT"]], "kT", ks)
                free["B_qkT"] = [s["kT"]]

            def stage_c(u):
                g, b = units[u]
                s = state[u]
                k = (first + u) % 2
                sc, sc_name = (B_out, "B_out") if small_heads and k else (B_sc, "B_sc")
                for r in range(R):
                    cols = slice(r * P, (r + 1) * P)
                    t = products(sc[:, cols], [((qT[0][:, cols], qT[1][:, cols]), (kT[0][:, :], kT[1][:, :]))],
                                 [s["qT"], s["kT"], *free[sc_name]], "scores" if r == R - 1 else None)
                free["qT"] = [t]
                s["sc"] = sc, sc_name, t

            def stage_c_mask(u):
                g, b = units[u]
                s = state[u]
                k = (first + u) % 2
                sc, sc_name, t = s["sc"]
                bank = sc[:, :].rearrange("p (r k) -> p r k", r=R)
                S3 = S[:, k, :].rearrange("p (r k) -> p r k", r=R)

                def per_head(m):
                    return m.unsqueeze(1).to_broadcast([P, R, P])

                if kind == "rope":
                    keep, minus = per_head(mask0[0][:, b, :]), per_head(mask0[1][:, b, :])
                    t = put("dve", lambda e: e.scalar_tensor_tensor(out=S3, in0=bank, scalar=scale, in1=keep, op0=ALU.mult,
                                                                    op1=ALU.mult), [t, t_mask0, *free[f"S{k}"]], "mask")
                    free[sc_name] = [t]
                    t = put("dve", lambda e: e.scalar_tensor_tensor(out=S3, in0=minus, scalar=-MASKED, in1=S3, op0=ALU.mult,
                                                                    op1=ALU.add), [t], "mask")
                    free["mask0"] = [t]
                else:
                    m = per_head(mask2 if small_heads else mask13[:, :])
                    t = put("dve", lambda e: e.scalar_tensor_tensor(out=S3, in0=bank, scalar=scale, in1=m, op0=ALU.mult,
                                                                    op1=ALU.add), [t, tokens["mask2"] if small_heads else t_m13, *free[f"S{k}"]], "mask")
                    free[sc_name] = [t]
                s["nmx"] = put("dve", lambda e: e.tensor_reduce(nmx[:, k, :], S3, AX, ALU.max, negate=True), [t], "max")

            def stage_c_exp(u):
                s = state[u]
                k = (first + u) % 2
                for r in range(R):
                    cols = slice(r * P, (r + 1) * P)
                    t = put("act", lambda e, r=r, cols=cols: e.activation(W[:, k, cols], S[:, k, cols], ACT.Exp,
                                                                         bias=nmx[:, k, r:r + 1],
                                                                         accum_out=den[:, k, r:r + 1]),
                            [s["nmx"], *free[f"W{k}"]] if r == 0 else (), "exp" if r == R - 1 else None)
                free[f"S{k}"] = [t]
                s["exp"] = t

            def stage_c_norm(u):
                s = state[u]
                k = (first + u) % 2
                t = put("dve", lambda e: e.reciprocal(rden[:, k, :], den[:, k, :]), [s["exp"]], "rden")
                W3 = W[:, k, :].rearrange("p (r k) -> p r k", r=R)
                s["p"] = put("pool", lambda e: e.tensor_tensor(W3, W3, rden[:, k, :].unsqueeze(2).to_broadcast([P, R, P]),
                                                               ALU.mult), [t], "probs")

            def stage_d(u):
                s = state[u]
                k = (first + u) % 2
                for r in range(R):
                    cols = slice(r * P, (r + 1) * P)
                    t = put("pe", lambda e, cols=cols: e.transpose(B_pt[:, cols], W[:, k, cols], ident[:, :]),
                            [s["p"], *free["B_pt"]] if r == 0 else (), "p_turn" if r == R - 1 else None)
                free[f"W{k}"] = [t]
                s["pT"] = split(B_pt[:, :], pT[0][:, :], pT[1][:, :], [t, *free["pT"]], "pT")
                free["B_pt"] = [s["pT"]]

            def stage_e(u):
                g, b = units[u]
                s = state[u]
                vs = (first + u) % VSLOTS
                begin, end = (g == 0, g == G - 1) if small_heads else (True, True)
                steps = [(v[0], pT[0]), (v[0], pT[1]), (v[1], pT[0])]
                for n, (a, c) in enumerate(steps):
                    t = put("pe", lambda e, a=a, c=c, n=n: e.matmul(B_oT[:, :], a[:, vs, :], c[:, :], start=begin and n == 0,
                                                                    stop=end and n == 2),
                            [s["pT"], s["v"], *(free["B_oT"] if begin else ())] if n == 0 else (), "pv" if n == 2 else None)
                free["pT"] = [t]
                free[f"v{vs}"] = [t]
                if end:
                    s["oT"] = split(B_oT[:, :], oT[0][:, :], oT[1][:, :], [t, *free["oT"]], "oT")
                    free["B_oT"] = [s["oT"]]

            def stage_f(u, now):
                g, b = units[u]
                if small_heads and g != G - 1:
                    return
                five, _, last = weights[u]
                (w0, tw0), (w1, tw1) = (piece(n) for n in five[3:5])
                pairs = [(tuple(m[:, r * P:(r + 1) * P] for m in oT),
                          tuple(m[:, (r % 2) * D:(r % 2 + 1) * D] for m in (w0, w1)[r // 2])) for r in range(R)]
                t = products(B_out[:, :], pairs, [state[u]["oT"], *tw0, *tw1, *free["B_out"]], "attn_out")
                free["oT"] = [t]
                if last:
                    for n in five[3:5]:
                        release(n, t, now)
                add_to_x(b, B_out, "B_out", gate, t)

            for u, (g, _) in enumerate(units):
                i = first + u
                at(i, 70, stage_a, u, i)
                if kind == "norm":
                    at(i + 1, 10, stage_a2, u)
                at(i + 1, 50, stage_b, u)
                at(i + 1 if g or not small_heads else i + 2, 50 if not small_heads else 41 if g else 8, stage_b_k, u)
                at(i + 2, 40, stage_c, u)
                at(i + 2, 42, stage_c_mask, u)
                if small_heads:
                    at(i + 3, 43, stage_c_exp, u)
                    at(i + 3, 45, stage_c_norm, u)
                else:
                    at(i + 2, 60, stage_c_exp, u)
                    at(i + 2, 65, stage_c_norm, u)
                at(i + lag_f - 2, 30, stage_d, u)
                at(i + lag_f - 1, 20, stage_e, u)
                at(i + lag_f, 0, stage_f, u, i + lag_f)
                if not small_heads and NB <= u < len(units) - NB:
                    steady.add(i)
            if small_heads:
                return [first + b * G + G - 1 + lag_f for b in range(NB)]
            return [first + units.index((G - 1, b)) + lag_f for b in range(NB)]

        def add_to_x(b, bank, bank_name, factor, token, after=()):
            t = put("dve", lambda e: e.scalar_tensor_tensor(out=X[:, b, :], in0=bank[:, :], scalar=factor, in1=X[:, b, :],
                                                            op0=ALU.mult, op1=ALU.add),
                    [token, x_done[b], t_tanh, *after], "x_add")
            free[bank_name] = [t]
            x_done[b] = t

        rt_done = [None]

        def chain(issue, *after):
            rt_done[0] = put("dve", issue, [rt_done[0], *after], "route")
            return rt_done[0]

        def first_max(onehot, top, src, n):
            chain(lambda e: e.tensor_reduce(top, src, AX, ALU.max))
            chain(lambda e: e.scalar_tensor_tensor(out=rt[:, 6, 0:n], in0=src, scalar=top, in1=rev[:, 0:n],
                                                   op0=ALU.is_equal, op1=ALU.mult), t_rev)
            yield
            chain(lambda e: e.tensor_reduce(r1[:, 15:16], rt[:, 6, 0:n], AX, ALU.max))
            chain(lambda e: e.tensor_scalar(onehot, rt[:, 6, 0:n], r1[:, 15:16], None, ALU.is_equal))

        def second_max(onehot2, top2, onehot1, src, n):
            chain(lambda e: e.scalar_tensor_tensor(out=rt[:, 5, 0:n], in0=onehot1, scalar=FAR, in1=src,
                                                   op0=ALU.mult, op1=ALU.add))
            yield from first_max(onehot2, top2, rt[:, 5, 0:n], n)

        def softmax_rows(dst, bank, n, token):
            t = chain(lambda e: e.tensor_reduce(r1[:, 0:1], bank, AX, ALU.max, negate=True), token)
            t = put("act", lambda e: e.activation(rt[:, 0, 0:n], bank, ACT.Exp, bias=r1[:, 0:1], accum_out=r1[:, 1:2]),
                    [t], "route_exp")
            chain(lambda e: e.reciprocal(r1[:, 2:3], r1[:, 1:2]), t)
            chain(lambda e: e.tensor_scalar(dst, rt[:, 0, 0:n], r1[:, 2:3], None, ALU.mult))
            return t

        def router_logits(b, first_col, n):
            def w(c):
                return tuple(m[:, CH * first_col + c * n:CH * first_col + (c + 1) * n] for m in routers)
            return products(B_sc[:, 0:n], [(xn_cols(c, b), w(c)) for c in range(CH)],
                            [xnT_ready[b], *arrive(router_items[0], 1), *free["B_sc"]], "logits")

        def ffn0(done_at, base):
            gate = gates[:, 4:5]
            hsT_state = {}
            weights = []
            weights += [need([base], done_at[0] + 1, 72) + need(range(base + 1, base + 4), done_at[0] + 2, 0)] * NB

            def low(b, now):
                (hg, t_hg) = piece(weights[b][0])
                t = products(B_sc[:, 0:HL + E0], [(xn_cols(c, b), tuple(m[:, c * (HL + E0):(c + 1) * (HL + E0)] for m in hg))
                                                  for c in range(CH)], [xnT_ready[b], *t_hg, *free["B_sc"]], "low_rank")
                if b == NB - 1:
                    release(weights[b][0], t, now + 0.7)
                t_h = put("act", act_copy(hs[:, b % 2, :], B_sc[:, 0:HL]), [t, *free[f"hs{b % 2}"]], "low_rank")
                free["B_sc"] = [chain(lambda e: e.tensor_copy(rt[:, 0, :], B_sc[:, HL:HL + E0]), t_h)]
                yield
                yield from first_max(rt[:, 1, :], r1[:, 0:1], rt[:, 0, :], E0)
                yield
                yield from second_max(rt[:, 2, :], r1[:, 1:2], rt[:, 1, :], rt[:, 0, :], E0)
                yield
                t = chain(lambda e: e.tensor_tensor(r1[:, 2:3], r1[:, 1:2], r1[:, 0:1], ALU.subtract))
                t = put("act", lambda e: e.activation(r1[:, 3:4], r1[:, 2:3], ACT.Exp), [t], "route_exp")
                yield
                chain(lambda e: e.tensor_scalar(r1[:, 4:5], r1[:, 3:4], 1.0, None, ALU.add), t)
                chain(lambda e: e.reciprocal(r1[:, 5:6], r1[:, 4:5]))
                chain(lambda e: e.tensor_tensor(r1[:, 6:7], r1[:, 3:4], r1[:, 5:6], ALU.mult))
                yield
                chain(lambda e: e.tensor_scalar(rt[:, 3, :], rt[:, 1, :], r1[:, 5:6], LORA_SCALE, ALU.mult, ALU.mult))
                chain(lambda e: e.tensor_scalar(rt[:, 4, :], rt[:, 2, :], r1[:, 6:7], LORA_SCALE, ALU.mult, ALU.mult))
                chain(lambda e: e.tensor_tensor(rt[:, 3, :], rt[:, 3, :], rt[:, 4, :], ALU.add))
                yield
                hs3 = hs[:, b % 2, :].rearrange("p (e r) -> p e r", r=RANK)
                t = chain(lambda e: e.tensor_tensor(hs3, hs3, rt[:, 3, :].unsqueeze(2).to_broadcast([P, E0, RANK]), ALU.mult))
                hsT_state[b] = t

            HH = HL // 2

            def turn(b):
                for k in range(2):
                    t = put("pe", lambda e, k=k: e.transpose(B_oT[0:HH, k * P:(k + 1) * P], hs[:, b % 2, k * HH:(k + 1) * HH],
                                                             ident[:, :]),
                            [hsT_state[b], *free["B_oT"]] if k == 0 else (), "hs_turn" if k == 1 else None)
                free[f"hs{b % 2}"] = [t]
                hsT_state["hsT"] = split(B_oT[0:HH, 0:2 * P], hsT[0][:, :], hsT[1][:, :],
                                         [t, *free["spare"]], "hsT")
                free["B_oT"] = [hsT_state["hsT"]]

            def out(b, now):
                (lb, t_lb), (w0, tw0), (w1, tw1) = (piece(n) for n in weights[b][1:])
                pairs = [(xn_cols(c, b), tuple(m[:, (c % 2) * D:(c % 2 + 1) * D] for m in (w0, w1)[c // 2])) for c in range(CH)]
                pairs += [(tuple(m[:, k * P:(k + 1) * P] for m in hsT), tuple(m[0:HH, k * D:(k + 1) * D] for m in lb))
                          for k in range(2)]
                t = products(B_out[:, :], pairs, [hsT_state["hsT"], *t_lb, *tw0, *tw1, *free["B_out"]], "ffn0")
                free["spare"] = [t]
                xnT_free[b] = t
                if b == NB - 1:
                    for n in weights[b][1:]:
                        release(n, t, now + 0.7)
                add_to_x(b, B_out, "B_out", gate, t)

            for b in range(NB):
                i = done_at[b]
                at(i, 12, ln_stats, b)
                at(i, 37, ln_apply, b)
                at(i + 1, 7, ln_turn, b)
                spread(i + 1, 72, low, b, i + 1)
                at(i + 3, 3, turn, b)
                at(i + 3, 66, out, b, i + 3)
            return [i + 4 for i in done_at]

        def ffn1(done_at, _):
            gate = gates[:, 5:6]
            weights = need(range(2), done_at[0] + 1, 67, "quantised")
            pick_ready = []

            def fill_pick():
                row, lo_row = (ident[0:LO_ROW + E3 + 1, c:c + 1].to_broadcast([LO_ROW + E3 + 1, P]) for c in (E3, LO_ROW + E3))
                pick_ready.append(put("dve", lambda e: e.tensor_tensor(pick1, row, lo_row, ALU.add),
                                      [t_ident, *free["spare"]], "pick"))

            def out(b, now):
                (w0, tw0), (w1, tw1) = (piece(n) for n in weights)
                pairs = [(xn_cols(c, b), tuple(m[:, (c % 2) * D:(c % 2 + 1) * D] for m in (w0, w1)[c // 2])) for c in range(CH)]
                t = products(B_out[:, :], pairs, [xnT_ready[b], *tw0, *tw1, t_biases, pick_ready[0], *free["B_out"]],
                             "ffn1", more=[(pick1, bias[:, :])])
                xnT_free[b] = t
                if b == NB - 1:
                    for n in weights:
                        release(n, t, now + 0.7)
                add_to_x(b, B_out, "B_out", gate, t)

            at(done_at[0], 1, fill_pick)
            for b in range(NB):
                i = done_at[b]
                at(i, 12, ln_stats, b)
                at(i, 37, ln_apply, b)
                at(i + 1, 7, ln_turn, b)
                at(i + 1, 67, out, b, i + 1)
            return [i + 2 for i in done_at]

        def ffn2(done_at, base):
            gate = gates[:, 6:7]
            comb_ready = [None] * NB

            def route(b):
                bank = B_sc[:, 0:E2]
                t = router_logits(b, 0, E2)
                t = softmax_rows(rt[:, 1, 0:E2], bank, E2, t)
                free["B_sc"] = [t]
                yield
                yield from first_max(rt[:, 2, 0:E2], r1[:, 3:4], rt[:, 1, 0:E2], E2)
                yield
                yield from second_max(rt[:, 3, 0:E2], r1[:, 4:5], rt[:, 2, 0:E2], rt[:, 1, 0:E2], E2)
                yield
                chain(lambda e: e.tensor_tensor(r1[:, 5:6], r1[:, 3:4], r1[:, 4:5], ALU.add))
                chain(lambda e: e.reciprocal(r1[:, 6:7], r1[:, 5:6]))
                chain(lambda e: e.tensor_scalar(r1[:, 7:8], r1[:, 3:4], r1[:, 6:7], gate, ALU.mult, ALU.mult), t_tanh)
                yield
                chain(lambda e: e.tensor_scalar(r1[:, 8:9], r1[:, 4:5], r1[:, 6:7], gate, ALU.mult, ALU.mult))
                chain(lambda e: e.tensor_scalar(rt[:, 4, 0:E2], rt[:, 3, 0:E2], r1[:, 8:9], None, ALU.mult))
                comb_ready[b] = chain(lambda e: e.scalar_tensor_tensor(out=comb[:, b, :], in0=rt[:, 2, 0:E2],
                                                                       scalar=r1[:, 7:8], in1=rt[:, 4, 0:E2],
                                                                       op0=ALU.mult, op1=ALU.add))

            experts = SHARED_TILES + E2
            steps = [(e + j, half) for e in range(0, experts, 2) for half in range(2) for j in range(2)]
            HB = NB // 2
            acts = [pT, oT]
            act_ready = {}
            banks = [(B_out, "B_out"), (B_sc, "B_sc"), (B_pt, "B_pt"), (B_oT, "B_oT")]

            def gu_piece(e):
                return weights[e // 2][e % 2]

            def up(n, now):
                e, half = steps[n]
                w, tw = piece(gu_piece(e))
                bank, name = ((B_qkv, "B_qkv"), (B_qkT, "B_qkT"))[n % 2]
                tokens = slice(half * HB * P, (half + 1) * HB * P)
                ready = xnT_ready[half * HB:(half + 1) * HB]
                tok = []
                for j in range(2):
                    wj = [tuple(m[:, c * 2 * P + j * P:c * 2 * P + (j + 1) * P] for m in w) for c in range(CH)]
                    tok.append(products(bank[:, j * 512:(j + 1) * 512], [(wj[c], tuple(m[:, c, tokens] for m in xnT))
                                                                         for c in range(CH)],
                                        [*tw, *ready, *free[name]], "gate_up"))
                if half == 1:
                    release(gu_piece(e), tok[1], now + 0.7)
                for b in range(half * HB, (half + 1) * HB):
                    xnT_free[b] = tok[1]
                k = n % 2
                th, sg = S[:, k, :], W[:, k, :]
                t = put("act", lambda e: e.activation(th, bank[:, 0:512], ACT.Tanh, scale=0.5), [tok[0], *free[f"S{k}"]], "silu")
                t = put("dve", lambda e: e.scalar_tensor_tensor(out=sg, in0=th, scalar=1.0, in1=bank[:, 0:512], op0=ALU.add,
                                                                op1=ALU.mult), [t, *free[f"W{k}"]], "silu")
                t = put("dve", lambda e: e.scalar_tensor_tensor(out=th, in0=sg, scalar=0.5, in1=bank[:, 512:1024],
                                                                op0=ALU.mult, op1=ALU.mult), [t, tok[1]], "act")
                free[name] = [t]
                free[f"W{k}"] = [t]
                dst = acts[k]
                h = put("act", act_copy(dst[0][:, :], th), [t, *free[("pT", "oT")[k]]], "act_hi")
                t = put("dve", sub(dst[1][:, :], th, f32(dst[0][:, :])), [h], "act_lo")
                free[f"S{k}"] = [t]
                act_ready[n] = t

            def down(n, now):
                e, half = steps[n]
                nd = weights[e // 2][2]
                w, tw = piece(nd)
                wd = tuple(m[:, (e % 2) * D:(e % 2 + 1) * D] for m in w)
                k = n % 2
                for j in range(HB):
                    b = half * HB + j
                    bank, name = banks[j]
                    t = products(bank[:, :], [(tuple(m[:, j * P:(j + 1) * P] for m in acts[k]), wd)],
                                 [act_ready[n], *tw, *free[name]], "down")
                    if e < SHARED_TILES:
                        add_to_x(b, bank, name, gate, t)
                    else:
                        add_to_x(b, bank, name, comb[:, b, e - SHARED_TILES:e - SHARED_TILES + 1], t, [comb_ready[b]])
                free[("pT", "oT")[k]] = [t]
                if half == 1 and e % 2 == 1:
                    release(nd, t, now + 0.7)

            for b in range(NB):
                at(done_at[b], 12, ln_stats, b)
                at(done_at[b], 37, ln_apply, b)
                at(done_at[b] + 1, 7, ln_turn, b)
                spread(done_at[b] + 1, 72, route, b)
            first = done_at[-1]
            weights = []
            for e in range(0, experts, 2):
                i, row = first + 2 * e, base + 3 * (e // 2)
                weights.append(need([row], i, 74) + need([row + 1], i + 1, 74) + need([row + 2], i + 1, 75))
            for n in range(len(steps)):
                at(first + n, 74, up, n, first + n)
                at(first + n + 1, 75, down, n, first + n + 1)
            return [first + len(steps) - 1 + b for b in range(NB)]

        def ffn3(done_at, base):
            gate = gates[:, 7:8]
            comb_ready = [None] * NB
            choice_ready, choiceT_ready = {}, {}
            banks = [(B_out, "B_out"), (B_oT, "B_oT"), (B_qkv[:, 0:D], "B_qkv"), (B_qkv[:, D:2 * D], "B_qkv second")]

            def route(b):
                t = router_logits(b, E2, E3)
                free["B_sc"] = [chain(lambda e: e.tensor_tensor(rt[:, 4, 0:E3], B_sc[:, 0:E3], gate_b[:, :], ALU.add),
                                      t, t_gate_b)]
                softmax_rows(rt[:, 1, 0:E3], rt[:, 4, 0:E3], E3, None)
                yield
                yield from first_max(rt[:, 2, 0:E3], r1[:, 3:4], rt[:, 1, 0:E3], E3)
                yield
                comb_ready[b] = chain(lambda e: e.tensor_scalar(comb[:, b, 0:E3], rt[:, 2, 0:E3], gate, None, ALU.mult),
                                      t_tanh)
                for row in (0, LO_ROW):
                    choice_ready[b] = chain(lambda e, row=row: e.tensor_copy(choice[:, row:row + E3], rt[:, 2, 0:E3]),
                                            *free["choice"])

            def clear_choice():
                chain(lambda e: e.memset(choice, 0.0), *free["hs0"])

            def turn_choice(b):
                t = put("pe", lambda e: e.transpose(B_pt[0:LO_ROW + E3 + 1, 0:P], choice, ident[:, :]),
                        [choice_ready[b], *free["B_pt"]], "choice_turn")
                free["choice"] = [t]
                choiceT_ready[b] = put("dve", lambda e: e.tensor_copy(choiceT, B_pt[0:LO_ROW + E3 + 1, 0:P]),
                                       [t, *free["choiceT"]], "choiceT")
                free["B_pt"] = [choiceT_ready[b]]

            def add_bias(b):
                t = products(B_oT[:, :], [], [choiceT_ready[b], t_biases, *free["B_oT"]], "bias3", more=[(choiceT, bias[:, :])])
                free["choiceT"] = [t]
                add_to_x(b, B_oT, "B_oT", gate, t)

            def expert(e3, b, now):
                (w0, tw0), (w1, tw1) = (piece(n) for n in weights[e3])
                pairs = [(xn_cols(c, b), tuple(m[:, (c % 2) * D:(c % 2 + 1) * D] for m in (w0, w1)[c // 2])) for c in range(CH)]
                if e3 == 0 and b == 0:
                    free["B_qkv second"] = free["B_qkv"]
                bank, name = banks[(2 * b + e3 % 2) % 4]
                t = products(bank[:, :], pairs, [*tw0, *tw1, *free[name]], "ffn3")
                if b == NB - 1:
                    for n in weights[e3]:
                        release(n, t, now + 0.7)
                add_to_x(b, bank, name, comb[:, b, e3:e3 + 1], t, [comb_ready[b]])

            for b in range(NB):
                at(done_at[b], 12, ln_stats, b)
                at(done_at[b], 37, ln_apply, b)
                at(done_at[b] + 1, 7, ln_turn, b)
                spread(done_at[b] + 1, 72, route, b)
                at(done_at[b] + 3, 3, turn_choice, b)
                at(done_at[b] + 3, 40, add_bias, b)
            at(done_at[0], 1, clear_choice)
            first = max(done_at[b] + 2 - b for b in range(NB))
            weights = []
            for e3 in range(0, E3, 2):
                for j in range(2):
                    row = base + 2 * (e3 + j)
                    weights.append(need([row, row + 1], first + e3 // 2 * NB, 74 + j))
                for b in range(NB):
                    i = first + e3 // 2 * NB + b
                    at(i, 74, expert, e3, b, i)
                    at(i, 75, expert, e3 + 1, b, i)
            return [first + (E3 // 2 - 1) * NB + b for b in range(NB)]

        ctx_items = {b: need([b], 1 + UNITS.index((0, b)), 70.5, "ctx")[0] for b in range(NB)}
        router_items = need([0], 40, 0, "routers")
        first, row = 1, 0
        done_at = [0] * NB
        for s in range(sublayers):
            layer = s // 2
            if s % 2 == 0:
                order = [b for b in range(NB) for _ in range(G)] if layer == 2 else [b for _, b in UNITS]
                if s:
                    first = max(first + G * NB, *(done_at[b] + 1 - order.index(b) for b in range(NB)))
                for b in range(NB):
                    i = max(done_at[b], first + order.index(b) - 2) if s else first + order.index(b) - 1
                    at(i, 12, ln_stats, b)
                    at(i, 37, ln_apply, b)
                    at(i + 1, 66 if layer == 2 and b > 1 else 7, ln_turn, b)
                done_at = attention(layer, first, row)
                row += 5 if layer == 2 else 5 * G
            else:
                done_at = (ffn0, ffn1, ffn2, ffn3)[layer](done_at, row)
                row += (4, 0, 3 * (SHARED_TILES + E2) // 2, 2 * E3)[layer]
        plan.sort(key=lambda x: x[:4])

        for b in range(1, NB):
            at(max(0, UNITS.index((0, b)) - 2), 1, load_x, b)

        fetch(-1)
        for n in range(7):
            split_next(None, ("pool", "dve")[n % 2])
            fetch(None)
        for i in range(1, max(events) + 1):
            for order in ((46, 90) if i in steady else (5, 24, 46, 90)):
                at(i, order, split_next, i + order / 100, "dve" if order == 46 else "pool")
                at(i, order, fetch, i + order / 100)
        for i in range(max(events) + 1):
            for _, _, what, args in sorted(events[i], key=lambda x: x[:2]):
                what(*args)
        assert not plan and not landing and all(next(parts, "end") == "end" for parts in finished)

        for b in range(NB):
            put("sync", lambda e, b=b: e.dma_start(out[b], X[:, b, :]), [x_done[b]], "store", 16)
        qs.wait_all("sync", ("sync_store", "sync_raw", "sync_scales", "sync_groupcols", "act_small", "pool_rope"))

        block = ctx.enter_context(nc.Block())
        block.sync(lambda e: qs.emit("sync", e))
        block.scalar(lambda e: qs.emit("act", e))
        block.vector(lambda e: qs.emit("dve", e))
        block.gpsimd(lambda e: qs.emit("pool", e))
        block.tensor(lambda e: qs.emit("pe", e))


def _chunks(w):
    return w.reshape(CH, P, -1).transpose(1, 0, 2)


def _two(w):
    return [w[:, 0:2].reshape(P, PIECE), w[:, 2:4].reshape(P, PIECE)]


def _pad(w):
    full = np.zeros((P, PIECE), np.float32)
    full[:w.shape[0], :w.shape[1]] = w
    return full


def _two_rows(w):
    full = np.zeros((LO_ROW + E3 + 1, w.shape[1]), np.float32)
    full[:E3 + 1] = full[LO_ROW:] = w
    return full


def _attention_pieces(wq, wk, wv, wo):
    out = []
    for g in range(wq.shape[1]):
        out += _two(_chunks(wq[:, g]))
        out.append(np.concatenate([_chunks(wk[:, g]), _chunks(wv[:, g])], axis=2).reshape(P, PIECE))
        out += _two(wo[g].transpose(1, 0, 2))
    return out


def _big(wq, wk, wv, wo):
    return _attention_pieces(wq.reshape(D, G, HG), wk.reshape(D, G, P), wv.reshape(D, G, P), wo.reshape(G, R, P, D))


def _layout(i):
    pieces = _big(i["L0_xattn_Wq"], i["L0_xattn_Wk"], i["L0_xattn_Wv"], i["L0_xattn_Wo"])
    low = np.concatenate([i["L0_ffn_lora_A"].reshape(HL, D).T, i["L0_ffn_gate_W"].T], axis=1)
    pieces.append(_pad(_chunks(low).reshape(P, -1)))
    lora_b = i["L0_ffn_lora_B"].transpose(0, 2, 1).reshape(2, HL // 2, D).transpose(1, 0, 2).reshape(HL // 2, 2 * D)
    pieces.append(_pad(lora_b))
    pieces += _two(_chunks(i["L0_ffn_base_W"].T))
    pieces += _big(*(i[f"L1_xattn_{k}_proj_w"].T for k in "qkvo"))
    hd = D // (G * R)
    wq = i["L2_xattn_w_q"].T.reshape(D, G, R, hd).transpose(0, 2, 1, 3).reshape(D, 1, D)
    wo = i["L2_xattn_w_out"].T.reshape(G, R, hd, D).transpose(1, 0, 2, 3).reshape(1, R, P, D)
    pieces += _attention_pieces(wq, i["L2_xattn_w_k"].T.reshape(D, 1, P), i["L2_xattn_w_v"].T.reshape(D, 1, P), wo)
    sgu, sdn = i["L2_ffn_shared_w_gate_up"], i["L2_ffn_shared_w_down"]
    gu = [np.concatenate([sgu[k * P:(k + 1) * P], sgu[D + k * P:D + (k + 1) * P]]).T for k in range(SHARED_TILES)]
    gu += [w.T for w in i["L2_ffn_w_gate_up"]]
    dn = [sdn[:, k * P:(k + 1) * P].T for k in range(SHARED_TILES)] + [w.T for w in i["L2_ffn_w_down"]]
    for e in range(0, SHARED_TILES + E2, 2):
        pieces += [_chunks(gu[e]).reshape(P, PIECE), _chunks(gu[e + 1]).reshape(P, PIECE),
                   np.concatenate([dn[e], dn[e + 1]], axis=1)]
    pieces += _big(*(i[f"L3_xattn_W{k}"].T for k in "qkvo"))
    for w in i["L3_ffn_expert_w"]:
        pieces += _two(_chunks(w.T))

    freq = (1.0 / THETA ** (np.arange(0, P, 2, dtype=np.float32) / np.float32(P))).astype(np.float32)
    angle = np.arange(MAX_POS, dtype=np.float32)[:, None] * freq[None, :]
    cos, sin = np.cos(angle), np.sin(angle)
    groups = np.arange(P) // hd

    def grouped(z):
        return np.stack(_two(_chunks(np.repeat(z.reshape(D, D // 32).T, 32, axis=0))))

    return {
        "pieces": np.stack(pieces),
        "ctxT": i["ctx_4096"].reshape(NB, P, CH, P).transpose(0, 3, 2, 1).reshape(NB, P, HALF),
        "routers": np.concatenate([_chunks(i["L2_ffn_gate_w"].T).reshape(P, -1),
                                   _chunks(i["L3_ffn_gate_w"].T).reshape(P, -1)], axis=1),
        "quant": np.stack(_two(_chunks(i["L1_ffn_qweight"].T))),
        "zeros": grouped(i["L1_ffn_zeros"]),
        "scales": grouped(i["L1_ffn_scales"]),
        "x": i["x"],
        "g_xattn": i["g_xattn"],
        "g_ffn": i["g_ffn"],
        "pos": i["pos_BxS2"].T,
        "mask0": i["mask_BxSxS2_ik0"].transpose(1, 0, 2).reshape(P, NB * P),
        "mask13": i["mask_1x1xSxS2_ff0"].reshape(P, P),
        "mask2": i["mask_SxS2_bk0"].view(np.int32),
        "norm_w": np.stack([i["L1_xattn_q_norm_w"], i["L3_xattn_q_norm_w"], i["L1_xattn_k_norm_w"],
                            i["L3_xattn_k_norm_w"]])[:, :, None],
        "bias": _two_rows(np.concatenate([i["L3_ffn_expert_b"], i["L1_ffn_bias"][None, :]])),
        "gate_b": i["L3_ffn_gate_b"],
        "rope": np.concatenate([cos, sin], axis=1).astype(np.float32),
        "ident": np.eye(P, dtype=np.float32),
        "groupmask": (groups[:, None] == np.arange(G)[None, :]).astype(np.float32),
        "groupcols": (groups[None, :] == np.arange(G)[:, None]).astype(np.float32).reshape(G * P),
        "rev": (E0 - np.arange(E0)).astype(np.float32),
    }


def kernel(sublayers=8, **inputs):
    import concourse.bacc as _bacc
    from concourse.bass_utils import run_bass_kernel_spmd as _run

    nc = _bacc.Bacc("TRN2", target_bir_lowering=False, num_devices=1)
    arrays = {f"in_{n}": np.ascontiguousarray(a) for n, a in _layout({k: np.asarray(v) for k, v in inputs.items()}).items()}
    io = {n[3:]: nc.dram_tensor(n, a.shape, mybir.dt.from_np(a.dtype), kind="ExternalInput").ap() for n, a in arrays.items()}
    io["groupcols"] = io["groupcols"].rearrange("(a n) -> a n", a=G)
    out = nc.dram_tensor("out_x", (NB, P, D), F32, kind="ExternalOutput").ap()
    build(nc, io, out, sublayers)
    r = _run(nc, [arrays], core_ids=[0])
    return r.results[0]["out_x"]
```
